# Optimizing a Trainium2 kernel written in Bass

```python
import numpy as np
import jax
import jax.numpy as jnp

def _softmax(x, axis=-1):
    return jax.nn.softmax(x, axis=axis)

def _gelu(x):
    return jax.nn.gelu(x, approximate=True)

def _silu(x):
    return jax.nn.silu(x)

def _sigmoid(x):
    return jax.nn.sigmoid(x)

def _layernorm(x, axis=-1, eps=1e-05):
    m = jnp.mean(x, axis=axis, keepdims=True)
    v = jnp.var(x, axis=axis, keepdims=True)
    return (x - m) / jnp.sqrt(v + eps)

def _scatter_add(tgt, idx, src, axis=0):
    return tgt.at[idx].add(src)

def _segment_sum(src, seg, n):
    return jax.ops.segment_sum(src, seg, n)
kernel_name = 'mk_flamingo_gated_d1_seqx_r4_957b65'

def setup_inputs(seed: int=0):
    np.random.seed(seed)
    _w = jnp.asarray

    def _rec_inputs():
        import jax
        import jax.numpy as jnp
        _rk = jax.random.key(seed)
        x = -0.000125 + 0.9999 * jax.random.normal(jax.random.fold_in(_rk, 1), (4, 512, 512), jnp.float32)
        _lenS = 512 - jax.random.randint(jax.random.fold_in(_rk, 7), (4,), 0, max(1, 512 // 4) + 1, jnp.int32)
        _lenS2 = 1601 - jax.random.randint(jax.random.fold_in(_rk, 8), (4,), 0, max(1, 1601 // 4) + 1, jnp.int32)
        _ctx_2048P = jax.random.normal(jax.random.fold_in(_rk, 11), (4, 16, 512), jnp.float32)
        _ctx_2048c = jax.random.dirichlet(jax.random.fold_in(_rk, 511), 0.3 * jnp.ones((16,), jnp.float32), (4, 1601))
        _ctx_2048t = jnp.einsum('bsk,bkd->bsd', _ctx_2048c, _ctx_2048P)
        _ctx_2048t = _ctx_2048t * jax.lax.rsqrt(jnp.mean(jnp.square(_ctx_2048t)) + 1e-12) * 0.953939
        ctx_2048 = 1.72703e-05 + 1.00003 * (_ctx_2048t + 0.3 * jax.random.normal(jax.random.fold_in(_rk, 611), (4, 1601, 512), jnp.float32))
        _g = jax.random.normal(jax.random.fold_in(_rk, 9001), (2, 1), jnp.float32)
        _g = jnp.sign(_g) * jnp.maximum(jnp.abs(_g), 1.0) + (_g == 0) * 1.0
        g_xattn = _g[0]
        g_ffn = _g[1]
        return (x, ctx_2048, g_xattn, g_ffn)
    x, ctx_2048, g_xattn, g_ffn = _rec_inputs()

    def _L0_xattn_setup():
        import jax, jax.numpy as jnp
        import numpy as np
        DIM = 512
        NH = 16
        HD = DIM // NH
        EPS = 1e-06
        IMG_LEN = 257

        def rms_norm(x, w, eps=EPS):
            xf = x.astype(jnp.float32)
            y = xf * jax.lax.rsqrt(jnp.mean(xf * xf, axis=-1, keepdims=True) + eps)
            return y.astype(x.dtype) * w

        def linear(x, w, b):
            return jnp.einsum('blc,oc->blo', x, w) + b

        def attention(q, k, v):
            scale = 1.0 / jnp.sqrt(jnp.asarray(HD, q.dtype))
            scores = jnp.einsum('bqhd,bkhd->bhqk', q, k) * scale
            probs = jax.nn.softmax(scores, axis=-1)
            return jnp.einsum('bhqk,bkhd->bqhd', probs, v)
        key = jax.random.key(seed)
        ks = jax.random.split(key, 12)
        B, L = (2, 2048)
        s = 0.02
        inp = {'x': jax.random.normal(ks[0], (B, L, DIM), jnp.float32), 'context': jax.random.normal(ks[1], (B, 769, DIM), jnp.float32), 'q_w': jax.random.normal(ks[2], (DIM, DIM), jnp.float32) * s, 'q_b': jnp.zeros((DIM,), jnp.float32), 'k_w': jax.random.normal(ks[3], (DIM, DIM), jnp.float32) * s, 'k_b': jnp.zeros((DIM,), jnp.float32), 'v_w': jax.random.normal(ks[4], (DIM, DIM), jnp.float32) * s, 'v_b': jnp.zeros((DIM,), jnp.float32), 'k_img_w': jax.random.normal(ks[5], (DIM, DIM), jnp.float32) * s, 'k_img_b': jnp.zeros((DIM,), jnp.float32), 'v_img_w': jax.random.normal(ks[6], (DIM, DIM), jnp.float32) * s, 'v_img_b': jnp.zeros((DIM,), jnp.float32), 'o_w': jax.random.normal(ks[7], (DIM, DIM), jnp.float32) * s, 'o_b': jnp.zeros((DIM,), jnp.float32), 'norm_q_w': jnp.ones((DIM,), jnp.float32), 'norm_k_w': jnp.ones((DIM,), jnp.float32), 'norm_k_img_w': jnp.ones((DIM,), jnp.float32)}
        return inp
    _L0_xattn_all = _L0_xattn_setup()
    _L0_xattn_in = {k: v for k, v in _L0_xattn_all.items() if k in ('q_w', 'q_b', 'k_w', 'k_b', 'v_w', 'v_b', 'k_img_w', 'k_img_b', 'v_img_w', 'v_img_b', 'o_w', 'o_b', 'norm_q_w', 'norm_k_w', 'norm_k_img_w')}
    del _L0_xattn_all

    def _L0_ffn_setup():
        import jax, jax.numpy as jnp
        import numpy as np
        H = 512
        E = 8
        TOPK = 2
        I_MOE = 256
        I_SH = 1024

        def _silu_and_mul(gu):
            g, u = jnp.split(gu, 2, axis=-1)
            return jax.nn.silu(g) * u
        key = jax.random.key(seed)
        ks = jax.random.split(key, 6)
        s = lambda *sh: 1.0 / np.sqrt(sh[-2])
        hidden_states = jax.random.normal(ks[0], (2, 256, H), dtype=jnp.float32)
        w_gate = jax.random.normal(ks[1], (H, E), dtype=jnp.float32) * (1.0 / np.sqrt(H))
        w_gate_up = jax.random.normal(ks[2], (E, H, 2 * I_MOE), dtype=jnp.float32) * (1.0 / np.sqrt(H))
        w_down = jax.random.normal(ks[3], (E, I_MOE, H), dtype=jnp.float32) * (1.0 / np.sqrt(I_MOE))
        w_sh_gate_up = jax.random.normal(ks[4], (H, 2 * I_SH), dtype=jnp.float32) * (1.0 / np.sqrt(H))
        w_sh_down = jax.random.normal(ks[5], (I_SH, H), dtype=jnp.float32) * (1.0 / np.sqrt(I_SH))
        return {'hidden_states': hidden_states, 'w_gate': w_gate, 'w_gate_up': w_gate_up, 'w_down': w_down, 'w_sh_gate_up': w_sh_gate_up, 'w_sh_down': w_sh_down}
    _L0_ffn_all = _L0_ffn_setup()
    _L0_ffn_in = {k: v for k, v in _L0_ffn_all.items() if k in ('w_gate', 'w_gate_up', 'w_down', 'w_sh_gate_up', 'w_sh_down')}
    del _L0_ffn_all
    return {'x': x, 'ctx_2048': ctx_2048, 'g_xattn': g_xattn, 'g_ffn': g_ffn, 'L0_xattn_q_w': _L0_xattn_in['q_w'], 'L0_xattn_q_b': _L0_xattn_in['q_b'], 'L0_xattn_k_w': _L0_xattn_in['k_w'], 'L0_xattn_k_b': _L0_xattn_in['k_b'], 'L0_xattn_v_w': _L0_xattn_in['v_w'], 'L0_xattn_v_b': _L0_xattn_in['v_b'], 'L0_xattn_k_img_w': _L0_xattn_in['k_img_w'], 'L0_xattn_k_img_b': _L0_xattn_in['k_img_b'], 'L0_xattn_v_img_w': _L0_xattn_in['v_img_w'], 'L0_xattn_v_img_b': _L0_xattn_in['v_img_b'], 'L0_xattn_o_w': _L0_xattn_in['o_w'], 'L0_xattn_o_b': _L0_xattn_in['o_b'], 'L0_xattn_norm_q_w': _L0_xattn_in['norm_q_w'], 'L0_xattn_norm_k_w': _L0_xattn_in['norm_k_w'], 'L0_xattn_norm_k_img_w': _L0_xattn_in['norm_k_img_w'], 'L0_ffn_w_gate': _L0_ffn_in['w_gate'], 'L0_ffn_w_gate_up': _L0_ffn_in['w_gate_up'], 'L0_ffn_w_down': _L0_ffn_in['w_down'], 'L0_ffn_w_sh_gate_up': _L0_ffn_in['w_sh_gate_up'], 'L0_ffn_w_sh_down': _L0_ffn_in['w_sh_down']}

def reference(x, ctx_2048, g_xattn, g_ffn, L0_xattn_q_w, L0_xattn_q_b, L0_xattn_k_w, L0_xattn_k_b, L0_xattn_v_w, L0_xattn_v_b, L0_xattn_k_img_w, L0_xattn_k_img_b, L0_xattn_v_img_w, L0_xattn_v_img_b, L0_xattn_o_w, L0_xattn_o_b, L0_xattn_norm_q_w, L0_xattn_norm_k_w, L0_xattn_norm_k_img_w, L0_ffn_w_gate, L0_ffn_w_gate_up, L0_ffn_w_down, L0_ffn_w_sh_gate_up, L0_ffn_w_sh_down):
    import jax
    import jax.numpy as jnp

    def _L0_xattn_ref(x, context, q_w, q_b, k_w, k_b, v_w, v_b, k_img_w, k_img_b, v_img_w, v_img_b, o_w, o_b, norm_q_w, norm_k_w, norm_k_img_w):
        import jax, jax.numpy as jnp
        import numpy as np
        DIM = 512
        NH = 16
        HD = DIM // NH
        EPS = 1e-06
        IMG_LEN = 257

        def rms_norm(x, w, eps=EPS):
            xf = x.astype(jnp.float32)
            y = xf * jax.lax.rsqrt(jnp.mean(xf * xf, axis=-1, keepdims=True) + eps)
            return y.astype(x.dtype) * w

        def linear(x, w, b):
            return jnp.einsum('blc,oc->blo', x, w) + b

        def attention(q, k, v):
            scale = 1.0 / jnp.sqrt(jnp.asarray(HD, q.dtype))
            scores = jnp.einsum('bqhd,bkhd->bhqk', q, k) * scale
            probs = jax.nn.softmax(scores, axis=-1)
            return jnp.einsum('bhqk,bkhd->bqhd', probs, v)
        B, L, _ = x.shape
        ctx_img = context[:, :IMG_LEN]
        ctx_txt = context[:, IMG_LEN:]
        q = rms_norm(linear(x, q_w, q_b), norm_q_w).reshape(B, L, NH, HD)
        k = rms_norm(linear(ctx_txt, k_w, k_b), norm_k_w).reshape(B, -1, NH, HD)
        v = linear(ctx_txt, v_w, v_b).reshape(B, -1, NH, HD)
        k_img = rms_norm(linear(ctx_img, k_img_w, k_img_b), norm_k_img_w).reshape(B, -1, NH, HD)
        v_img = linear(ctx_img, v_img_w, v_img_b).reshape(B, -1, NH, HD)
        img_x = attention(q, k_img, v_img)
        txt_x = attention(q, k, v)
        out = (txt_x + img_x).reshape(B, L, DIM)
        return linear(out, o_w, o_b)

    def _L0_ffn_ref(hidden_states, w_gate, w_gate_up, w_down, w_sh_gate_up, w_sh_down):
        import jax, jax.numpy as jnp
        import numpy as np
        H = 512
        E = 8
        TOPK = 2
        I_MOE = 256
        I_SH = 1024

        def _silu_and_mul(gu):
            g, u = jnp.split(gu, 2, axis=-1)
            return jax.nn.silu(g) * u
        orig_shape = hidden_states.shape
        x = hidden_states.reshape(-1, orig_shape[-1])
        router_logits = x @ w_gate
        probs = jax.nn.softmax(router_logits, axis=-1)
        topk_w, topk_ids = jax.lax.top_k(probs, TOPK)
        topk_w = topk_w / jnp.sum(topk_w, axis=-1, keepdims=True)
        combine = jnp.sum(topk_w[..., None] * jax.nn.one_hot(topk_ids, E, dtype=x.dtype), axis=1)
        gu = jnp.einsum('th,ehf->etf', x, w_gate_up)
        act = _silu_and_mul(gu)
        eo = jnp.einsum('eti,eih->eth', act, w_down)
        routed = jnp.einsum('te,eth->th', combine, eo)
        shared = _silu_and_mul(x @ w_sh_gate_up) @ w_sh_down
        return (routed + shared).reshape(orig_shape)
    x = x + jnp.tanh(g_xattn[0]) * _L0_xattn_ref(_layernorm(x, axis=-1), ctx_2048, L0_xattn_q_w, L0_xattn_q_b, L0_xattn_k_w, L0_xattn_k_b, L0_xattn_v_w, L0_xattn_v_b, L0_xattn_k_img_w, L0_xattn_k_img_b, L0_xattn_v_img_w, L0_xattn_v_img_b, L0_xattn_o_w, L0_xattn_o_b, L0_xattn_norm_q_w, L0_xattn_norm_k_w, L0_xattn_norm_k_img_w)
    x = x + jnp.tanh(g_ffn[0]) * _L0_ffn_ref(_layernorm(x, axis=-1), L0_ffn_w_gate, L0_ffn_w_gate_up, L0_ffn_w_down, L0_ffn_w_sh_gate_up, L0_ffn_w_sh_down)
    return x

_drawn_inputs = setup_inputs


def setup_inputs(seed=0):
    import zlib

    import numpy as np

    out = dict(_drawn_inputs(seed))
    spreads = {'L0_xattn_q_b': (0.0, 0.365),
     'L0_xattn_k_b': (0.0, 0.8),
     'L0_xattn_v_b': (0.0, 0.1),
     'L0_xattn_k_img_b': (0.0, 0.8),
     'L0_xattn_v_img_b': (0.0, 0.1),
     'L0_xattn_o_b': (0.0, 0.1),
     'L0_xattn_norm_q_w': (1.0, 0.6),
     'L0_xattn_norm_k_w': (1.0, 0.6),
     'L0_xattn_norm_k_img_w': (1.0, 0.6)}
    factors = {}
    for name, (base, spread) in spreads.items():
        noise = np.random.default_rng([zlib.crc32(name.encode()), seed]).standard_normal(out[name].shape)
        drawn = base * np.exp(spread * noise) if base else spread * noise
        out[name] = jnp.asarray(drawn.astype(out[name].dtype))
    for name, factor in factors.items():
        out[name] = (out[name] * factor).astype(out[name].dtype)
    return out
```

```python
import numpy as np
from contextlib import ExitStack

import concourse.bass as bass
from concourse import mybir

F32 = mybir.dt.float32
F32R = mybir.dt.float32r
U32 = mybir.dt.uint32
ACT = mybir.ActivationFunctionType
ALU = mybir.AluOpType
AX = mybir.AxisListType

NB = 4
D = 512
LQ = 512
NTXT, NIMG = 1344, 257
NK = NTXT + NIMG
NKP = NK + 1
NKT = 13
SCALE = 1.0 / float(np.sqrt(np.float32(32.0)))
NE = 8


class Queue:

    def __init__(self, eng, sem):
        self.eng, self.sem, self.n, self.seen = eng, sem, 0, {}

    def wait(self, *handles):
        for h in handles:
            if h is not None and self.seen.get(h[0].name, 0) < h[1]:
                self.eng.wait_ge(*h)
                self.seen[h[0].name] = h[1]

    def do(self, fn, *waits, mark=True):
        self.wait(*waits)
        ins = fn(self.eng)
        if mark:
            ins.then_inc(self.sem, 1)
            self.n += 1
            return (self.sem, self.n)
        return None

    def dma(self, slot, fn, *waits):
        self.wait(*waits)
        fn(self.eng).then_inc(slot.sem, 16)
        slot.n += 16
        return (slot.sem, slot.n)


class Slot:

    def __init__(self, sem):
        self.sem, self.n = sem, 0


class Banks:

    def __init__(self, banks):
        self.banks, self.at, self.readers = banks, 0, [[] for _ in banks]

    def take(self):
        i = self.at % len(self.banks)
        self.at += 1
        r, self.readers[i] = self.readers[i], []
        return self.banks[i], i, r

    def read_by(self, i, handle):
        self.readers[i].append(handle)


def flamingo_program(nc, ap):
    ctx = ExitStack()
    with ctx:
        def sem(name):
            return ctx.enter_context(nc.semaphore(name))

        PE, DVE, ACTQ, POOL, SP = (Queue(e, sem(n)) for e, n in (
            (nc.tensor, "c_pe"), (nc.vector, "c_dve"), (nc.scalar, "c_act"), (nc.gpsimd, "c_pool"), (nc.sync, "c_sp")))
        slots = []

        def slot(name):
            slots.append(Slot(sem(name)))
            return slots[-1]

        def sb(stack, name, shape, dt):
            return stack.enter_context(nc.sbuf_tensor(name, shape, dt))

        ps = ctx.enter_context(nc.psum_tensor("ps", [128, 8, 512], F32))

        KHd = nc.dram_tensor("KHd", (NB, D, NKP), F32).ap()
        KLd = nc.dram_tensor("KLd", (NB, D, NKP), F32).ap()
        Vd = nc.dram_tensor("Vd", (NB, NK, D), F32).ap()
        QHd = nc.dram_tensor("QHd", (NB, D, LQ), F32).ap()
        QLd = nc.dram_tensor("QLd", (NB, D, LQ), F32).ap()

        def barrier():
            h = [(q.sem, q.n) for q in (PE, DVE, ACTQ, POOL) if q.n] + [(s.sem, s.n) for s in slots if s.n]
            for q in (PE, DVE, ACTQ, POOL, SP):
                q.wait(*h)

        def three(out, ah, al, bh, bl, first, last, *waits):
            PE.do(lambda e: e.matmul(out, ah, bh, start=first, stop=False), *waits, mark=False)
            PE.do(lambda e: e.matmul(out, ah, bl, start=False, stop=False), mark=False)
            return PE.do(lambda e: e.matmul(out, al, bh, start=False, stop=last), mark=last)

        ident = sb(ctx, "ident", [128, 128], F32)
        acc = sb(ctx, "acc", [128, 16, D], F32)
        tg = sb(ctx, "tg", [128, 2], F32)
        gin = sb(ctx, "gin", [128, 2], F32)
        s_c = slot("s_c")
        h_id = SP.dma(s_c, lambda e: e.dma_start(ident[:], ap["ident"]))
        SP.dma(s_c, lambda e: e.dma_start(gin[:, 0:1], ap["g_xattn"].partition_broadcast(128)))
        h_g = SP.dma(s_c, lambda e: e.dma_start(gin[:, 1:2], ap["g_ffn"].partition_broadcast(128)))
        h_id = h_g
        h_tg = ACTQ.do(lambda e: e.activation(tg[:], gin[:], ACT.Tanh), h_g)

        p1 = ExitStack()
        bias = sb(p1, "bias", [128, 8, D], F32)
        QB, QNW, KB, KNW, VB, KIB, KINW, VIB = range(8)
        Wh = sb(p1, "Wh", [128, 5, 4, D], F32R)
        Wl = sb(p1, "Wl", [128, 5, 4, D], F32R)
        wraw = sb(p1, "wraw", [128, 4, D], F32)
        raw = sb(p1, "raw", [128, 2, 4, 256], F32)
        ch = sb(p1, "ch", [128, 2, 4, 256], F32R)
        cl = sb(p1, "cl", [128, 2, 4, 256], F32R)
        kf = sb(p1, "kf", [128, 3, D], F32)
        vf = sb(p1, "vf", [128, 3, D], F32)
        junk = sb(p1, "junk", [128, D], F32)
        sth = sb(p1, "sth", [128, 2, 4, 258], F32R)
        stl = sb(p1, "stl", [128, 2, 4, 258], F32R)
        xn = sb(p1, "xn", [128, 2, D], F32)
        st = sb(p1, "st", [128, 8, 8], F32)
        bst = sb(p1, "bst", [128, 2, 6], F32)
        mv = sb(p1, "mv", [128, 2, 2], F32)

        s_b, s_x, s_w = slot("s_b"), slot("s_x"), slot("s_w")
        s_raw = [slot(f"s_raw{i}") for i in range(2)]
        s_st = [slot(f"s_st{i}") for i in range(2)]
        s_v = [slot(f"s_v{i}") for i in range(3)]

        names = ["q_b", "norm_q_w", "k_b", "norm_k_w", "v_b", "k_img_b", "norm_k_img_w", "v_img_b"]
        for i, n in enumerate(names):
            h_bias = SP.dma(s_b, lambda e, i=i, n=n: e.dma_start(bias[:, i, :], ap[n].partition_broadcast(128)))
        xv = ap["x"].rearrange("b (t p) d -> p (b t) d", p=128)
        WQ, WK, WV, WKI, WVI = range(5)
        wsplit, wfree = {}, None

        def load_w(w, name):
            nonlocal wfree
            h = SP.dma(s_w, lambda e: e.dma_start(wraw[:], ap[name].rearrange("(k p) o -> p k o", p=128)), wfree)
            hh = ACTQ.do(lambda e: e.activation(Wh[:, w], wraw[:], ACT.Copy), h)
            hl = DVE.do(lambda e: e.tensor_sub(Wl[:, w], wraw[:], Wh[:, w].bitcast(F32)), h, hh)
            wfree = hl
            wsplit[w] = (hh, hl)

        load_w(WQ, "q_wT")
        h_x = []
        for b in range(NB):
            h_x.append(SP.dma(s_x, lambda e, b=b: e.dma_start(acc[:, 4 * b:4 * b + 4, :], xv[:, 4 * b:4 * b + 4, :])))
        h_x = [h_x[-1]] * NB
        for w, n in ((WK, "k_wT"), (WV, "v_wT"), (WKI, "k_img_wT"), (WVI, "v_img_wT")):
            load_w(w, n)

        mm, tr = Banks(range(0, 6)), Banks(range(6, 8))
        nst = 0
        st_last = [None] * 8

        def rms(src, rows, row_wait, nw):
            nonlocal nst
            r = nst % 8
            nst += 1
            a = ACTQ.do(lambda e: e.activation(junk[:rows], src, ACT.Square, accum_out=st[:rows, r, 0:1]),
                        row_wait, st_last[r], (ACTQ.sem, ACTQ.n) if ACTQ.n else None)
            b_ = DVE.do(lambda e: e.tensor_scalar(st[:rows, r, 1:2], st[:rows, r, 0:1], 1.0 / D, 1e-6, ALU.mult, ALU.add), a)
            c = ACTQ.do(lambda e: e.activation(st[:rows, r, 2:3], st[:rows, r, 1:2], ACT.Sqrt), b_)
            d = DVE.do(lambda e: e.reciprocal(st[:rows, r, 3:4], st[:rows, r, 2:3]), c)
            h = DVE.do(lambda e: e.scalar_tensor_tensor(src, src, st[:rows, r, 3:4], bias[:rows, nw, :], ALU.mult, ALU.mult), d)
            st_last[r] = h
            return h

        kf_free, vf_free = [None] * 3, [None] * 3
        st_free = [[] for _ in range(2)]
        nkf = nvf = 0

        def transposed(src, rows, src_wait, hi, lo, dst_waits, extra=False):
            bank, i, free = tr.take()
            for g in range(4):
                h = PE.do(lambda e, g=g: e.transpose(ps[:, bank, g * 128:g * 128 + rows], src[:, g * 128:g * 128 + 128], ident[:rows, :rows]),
                          src_wait, h_id, *free, mark=(g == 3))
            v = ps[:, bank, :].rearrange("p (g s) -> p g s", g=4)[:, :, 0:rows]
            a = ACTQ.do(lambda e: e.activation(hi, v, ACT.Copy), h, *dst_waits)
            d = DVE.do(lambda e: e.tensor_sub(lo, v, hi.bitcast(F32)), a, *dst_waits)
            tr.read_by(i, a)
            tr.read_by(i, d)
            return a, d, h

        xn_free = [None] * 2
        ch_free = [None] * 2
        q_pending = []

        q_done = []

        def finish_q(b, t, slot3, hnorm):
            s, c0 = (t // 2) % 2, 128 * (t % 2)
            a, d, ht = transposed(kf[:, slot3, :], 128, hnorm, sth[:, s, :, c0:c0 + 128], stl[:, s, :, c0:c0 + 128], st_free[s])
            kf_free[slot3] = ht
            q_done.extend([a, d])
            if t % 2:
                for src, dst in ((sth, QHd), (stl, QLd)):
                    st_free[s] = [POOL.dma(s_st[s], lambda e, src=src, dst=dst: e.dma_start(
                        dst[b].rearrange("(k p) s -> p k s", p=128)[:, :, 256 * s:256 * s + 256], src[:, s, :, 0:256].bitcast(F32)), *q_done)]
                q_done.clear()

        for b in range(NB):
            for t in range(4):
                k = 4 * b + t
                xs = k % 2
                a = DVE.do(lambda e, k=k, xs=xs: e.bn_stats(bst[:, xs, :], acc[:, k, :]), h_x[b])
                a = DVE.do(lambda e, xs=xs: e.bn_aggr(mv[:, xs, :], bst[:, xs, :]), a)
                r = nst % 8
                nst += 1
                a = DVE.do(lambda e, xs=xs, r=r: e.tensor_scalar(st[:, r, 1:2], mv[:, xs, 1:2], 1e-5, None, ALU.add), a, st_last[r])
                c = ACTQ.do(lambda e, r=r: e.activation(st[:, r, 2:3], st[:, r, 1:2], ACT.Sqrt), a)
                d = DVE.do(lambda e, r=r: e.reciprocal(st[:, r, 3:4], st[:, r, 2:3]), c)
                d = DVE.do(lambda e, k=k, xs=xs, r=r: e.tensor_scalar(xn[:, xs, :], acc[:, k, :], mv[:, xs, 0:1], st[:, r, 3:4], ALU.subtract, ALU.mult), d, xn_free[xs])
                st_last[r] = d
                xh, xl = ch[:, xs, :, 0:128], cl[:, xs, :, 0:128]
                a, d, ht = transposed(xn[:, xs, :], 128, d, xh, xl, [ch_free[xs]])
                xn_free[xs] = ht
                if q_pending:
                    finish_q(*q_pending.pop())
                bank, i, free = mm.take()
                for kk in range(4):
                    hq = three(ps[:, bank, :], xh[:, kk], xl[:, kk], Wh[:, WQ, kk, :], Wl[:, WQ, kk, :], kk == 0, kk == 3, a, d, *wsplit[WQ], *free)
                ch_free[xs] = hq
                s3 = nkf % 3
                nkf += 1
                h = DVE.do(lambda e, s3=s3, bank=bank: e.tensor_tensor(kf[:, s3, :], ps[:, bank, :], bias[:, QB, :], ALU.add), hq, h_bias, kf_free[s3])
                mm.read_by(i, h)
                h = rms(kf[:, s3, :], 128, h, QNW)
                q_pending.append((b, t, s3, h))
        finish_q(*q_pending.pop())

        raw_free = [[] for _ in range(2)]
        ctf = ap["ctxT"]
        k_pending = []
        nchunk = 0

        def finish_k(b, c, j, rows, s, s3, hnorm, last, width):
            c0 = 128 * j
            a, d, ht = transposed(kf[:rows, s3, :], rows, hnorm, sth[:, s, :, c0:c0 + rows], stl[:, s, :, c0:c0 + rows], st_free[s])
            kf_free[s3] = ht
            k_done.extend([a, d])
            if c == 6:
                for q, dst in ((ACTQ, sth), (DVE, stl)):
                    if q is ACTQ:
                        k_done.append(q.do(lambda e, dst=dst: e.activation(dst[:, s, :, rows:rows + 1], dst[:, s, :, rows - 1:rows].bitcast(F32), ACT.Copy), a))
                    else:
                        k_done.append(q.do(lambda e, dst=dst: e.tensor_copy(dst[:, s, :, rows:rows + 1], dst[:, s, :, rows - 1:rows].bitcast(F32)), d))
            if last:
                for src, dst in ((sth, KHd), (stl, KLd)):
                    st_free[s] = [POOL.dma(s_st[s], lambda e, src=src, dst=dst: e.dma_start(
                        dst[b].rearrange("(k p) s -> p k s", p=128)[:, :, 256 * c:256 * c + width],
                        src[:, s, :, 0:width].bitcast(F32)), *k_done)]
                k_done.clear()

        k_done = []
        for b in range(NB):
            for c in range(7):
                n = 256 if c < 6 else 65
                s = nchunk % 2
                nchunk += 1
                h = SP.dma(s_raw[s], lambda e, b=b, c=c, n=n, s=s: e.dma_start(
                    raw[:, s, :, 0:n], ctf[b].rearrange("(k p) s -> p k s", p=128)[:, :, 256 * c:256 * c + n]), *raw_free[s])
                hh = ACTQ.do(lambda e, n=n, s=s: e.activation(ch[:, s, :, 0:n], raw[:, s, :, 0:n], ACT.Copy), h, ch_free[s])
                hl = POOL.do(lambda e, n=n, s=s: e.tensor_tensor(cl[:, s, :, 0:n], raw[:, s, :, 0:n], ch[:, s, :, 0:n].bitcast(F32), ALU.subtract), h, hh, ch_free[s])
                raw_free[s] = [hh, hl]
                for j in range(2 if c < 6 else 1):
                    rows = 128 if c < 6 else 65
                    t = 2 * c + j
                    if t < 10:
                        parts = [(0, 128, WK, WV, KB, KNW, VB)]
                    elif t == 10:
                        parts = [(0, 64, WK, WV, KB, KNW, VB), (64, 128, WKI, WVI, KIB, KINW, VIB)]
                    else:
                        parts = [(0, rows, WKI, WVI, KIB, KINW, VIB)]
                    s3 = nkf % 3
                    nkf += 1
                    hk = []
                    for p0, p1_, wk, wv, kb, knw, vb in parts:
                        bank, i, free = mm.take()
                        for kk in range(4):
                            hm = three(ps[:rows, bank, :], ch[:, s, kk, 128 * j:128 * j + rows], cl[:, s, kk, 128 * j:128 * j + rows],
                                       Wh[:, wk, kk, :], Wl[:, wk, kk, :], kk == 0, kk == 3, hh, hl, *wsplit[wk], *free)
                        h = DVE.do(lambda e, s3=s3, bank=bank, p0=p0, p1_=p1_, kb=kb: e.tensor_tensor(
                            kf[p0:p1_, s3, :], ps[p0:p1_, bank, :], bias[p0:p1_, kb, :], ALU.add), hm, kf_free[s3])
                        mm.read_by(i, h)
                        hk.append(h)
                    if len(parts) == 2:
                        r = nst % 8
                        nst += 1
                        a = ACTQ.do(lambda e, s3=s3, r=r: e.activation(junk[:], kf[:, s3, :], ACT.Square, accum_out=st[:, r, 0:1]), hk[-1], st_last[r], (ACTQ.sem, ACTQ.n))
                        a = DVE.do(lambda e, r=r: e.tensor_scalar(st[:, r, 1:2], st[:, r, 0:1], 1.0 / D, 1e-6, ALU.mult, ALU.add), a)
                        a = ACTQ.do(lambda e, r=r: e.activation(st[:, r, 2:3], st[:, r, 1:2], ACT.Sqrt), a)
                        d = DVE.do(lambda e, r=r: e.reciprocal(st[:, r, 3:4], st[:, r, 2:3]), a)
                        for p0, p1_, nw in ((0, 64, KNW), (64, 128, KINW)):
                            hn = DVE.do(lambda e, s3=s3, r=r, p0=p0, p1_=p1_, nw=nw: e.scalar_tensor_tensor(
                                kf[p0:p1_, s3, :], kf[p0:p1_, s3, :], st[p0:p1_, r, 3:4], bias[p0:p1_, nw, :], ALU.mult, ALU.mult), d)
                        st_last[r] = hn
                    else:
                        hn = rms(kf[:rows, s3, :], rows, hk[-1], parts[0][5])
                    if k_pending:
                        finish_k(*k_pending.pop())
                    sv = nvf % 3
                    nvf += 1
                    for p0, p1_, wk, wv, kb, knw, vb in parts:
                        bank, i, free = mm.take()
                        for kk in range(4):
                            hm = three(ps[:rows, bank, :], ch[:, s, kk, 128 * j:128 * j + rows], cl[:, s, kk, 128 * j:128 * j + rows],
                                       Wh[:, wv, kk, :], Wl[:, wv, kk, :], kk == 0, kk == 3, *wsplit[wv], *free)
                        h = DVE.do(lambda e, sv=sv, bank=bank, p0=p0, p1_=p1_, vb=vb: e.tensor_tensor(
                            vf[p0:p1_, sv, :], ps[p0:p1_, bank, :], bias[p0:p1_, vb, :], ALU.add), hm, vf_free[sv])
                        mm.read_by(i, h)
                    vf_free[sv] = POOL.dma(s_v[sv], lambda e, b=b, t=t, rows=rows, sv=sv: e.dma_start(
                        Vd[b, 128 * t:128 * t + rows, :], vf[:rows, sv, :]), h)
                    ch_free[s] = hm
                    k_pending.append((b, c, j, rows, s, s3, hn, j == 1 or c == 6, n if c < 6 else 66))
        finish_k(*k_pending.pop())
        p1.close()
        barrier()

        p2 = ExitStack()
        Kst = [sb(p2, f"Kst{i}", [128, 4, NKP], F32R) for i in range(2)]
        Qst = [sb(p2, f"Qst{i}", [128, 4, LQ], F32R) for i in range(2)]
        Vg = [sb(p2, f"Vg{i}", [128, NKT, 128], F32) for i in range(2)]
        P = [sb(p2, f"P{i}", [128, 4, LQ], F32) for i in range(3)]
        aTh = sb(p2, "aTh", [128, 4, LQ], F32R)
        aTl = sb(p2, "aTl", [128, 4, LQ], F32R)
        Woh = sb(p2, "Woh", [128, 4, D], F32R)
        Wol = sb(p2, "Wol", [128, 4, D], F32R)
        woraw = sb(p2, "woraw", [128, 4, D], F32)
        obb = sb(p2, "obb", [128, D], F32)
        rt = sb(p2, "rt", [128, D], F32)
        ot = sb(p2, "ot", [128, D], F32)
        oi = sb(p2, "oi", [128, D], F32)
        ones = sb(p2, "ones", [128, 32], F32)
        mp = sb(p2, "mp", [128, 16, 4], F32)
        mx = sb(p2, "mx", [128, 16, 2], F32)
        mn = sb(p2, "mn", [128, 16, 4], F32R)
        mrow = sb(p2, "mrow", [16, LQ], F32R)
        ind = sb(p2, "ind", [128, NKP], F32)

        s_k2 = [slot(f"s_k2{i}") for i in range(2)]
        s_q2 = [slot(f"s_q2{i}") for i in range(2)]
        s_v2 = [slot(f"s_v2{i}") for i in range(2)]
        s_m2 = [slot(f"s_m2{i}") for i in range(2)]
        s_c2 = slot("s_c2")

        NG = 4 * NB
        kst_free = [[] for _ in range(2)]
        qst_free = [[] for _ in range(2)]
        vg_free = [[] for _ in range(2)]
        h_k, h_q, h_v = {}, {}, {}

        h_ind = SP.dma(s_c2, lambda e: e.dma_start(ind[96:100, :], ap["ind"]))

        def load_group(G):
            b, g, s = G // 4, G % 4, G % 2
            rows = slice(128 * g, 128 * g + 128)

            def head_rows(d):
                return d[b, rows, :].rearrange("(j p) s -> p j s", p=32)
            for p0, d in ((0, QHd), (32, QLd), (64, QHd)):
                h_q[G] = SP.dma(s_q2[s], lambda e, p0=p0, d=d: e.dma_start(Qst[s][p0:p0 + 32].bitcast(F32), head_rows(d)), *qst_free[s])
            for p0, d in ((0, KHd), (32, KHd), (64, KLd)):
                h_k[G] = SP.dma(s_k2[s], lambda e, p0=p0, d=d: e.dma_start(Kst[s][p0:p0 + 32].bitcast(F32), head_rows(d)), *kst_free[s])
            SP.dma(s_v2[s], lambda e: e.dma_start(
                Vg[s][:, 0:12, :], Vd[b, 0:1536, rows].rearrange("(t p) d -> p t d", p=128)), *vg_free[s])
            h_v[G] = SP.dma(s_v2[s], lambda e: e.dma_start(Vg[s][0:65, 12, :], Vd[b, 1536:NK, rows]))

        load_group(0)
        h_wo = SP.dma(s_c2, lambda e: e.dma_start(woraw[:], ap["o_wT"].rearrange("(k p) o -> p k o", p=128)))
        h_ob = SP.dma(s_c2, lambda e: e.dma_start(obb[:], ap["o_b"].partition_broadcast(128)))
        h_ind = h_wo = h_ob
        load_group(1)
        h_ones = DVE.do(lambda e: e.memset(ones[:], 1.0))
        hi_ = []
        for s in range(2):
            for j in range(4):
                hi_.append(ACTQ.do(lambda e, s=s, j=j: e.activation(Kst[s][96:100, j, :], ind[96:100, :], ACT.Copy), h_ind))
        h_indk = hi_[-1]
        a = ACTQ.do(lambda e: e.activation(Woh[:], woraw[:], ACT.Copy), h_wo)
        h_wos = DVE.do(lambda e: e.tensor_sub(Wol[:], woraw[:], Woh[:].bitcast(F32)), a)
        h_xb = []
        for k in range(16):
            h_xb.append(DVE.do(lambda e, k=k: e.scalar_tensor_tensor(acc[:, k, :], obb[:], tg[:, 0:1], acc[:, k, :], ALU.mult, ALU.add), h_ob, h_tg))

        ra, rb = Banks([0, 1]), Banks([2, 4])
        CH = [(0, 512), (512, 1024), (1024, NTXT), (NTXT, NKP)]
        mdone = {}

        def max_units(G):
            s = G % 2
            last = {}
            units = []
            for qt in range(4):
                for j in range(4):
                    for c, (c0, c1) in enumerate(CH):
                        def unit(qt=qt, j=j, c=c, c0=c0, c1=c1):
                            bank, i, free = ra.take()
                            h = PE.do(lambda e: e.matmul(ps[:, bank, 0:c1 - c0], Qst[s][0:96, j, 128 * qt:128 * qt + 128],
                                                         Kst[s][0:96, j, c0:c1], start=True, stop=True), h_k[G], h_q[G], *free)
                            h = DVE.do(lambda e: e.reduce_max(mp[:, 4 * qt + j, c:c + 1], ps[:, bank, 0:c1 - c0], AX.X), h, last.get("mpfree"))
                            ra.read_by(i, h)
                            last["h"] = h
                            last["pe"] = (PE.sem, PE.n)
                        units.append(unit)

            def rows_of_m():
                a = DVE.do(lambda e: e.tensor_reduce(mx[:, :, 0], mp[:, :, 0:3], axis=AX.X, op=ALU.max), last["h"], mdone.get(("mn", G - 1)))
                b_ = DVE.do(lambda e: e.tensor_copy(mx[:, :, 1], mp[:, :, 3]), last["h"])
                hs = []
                for k in range(2):
                    c = DVE.do(lambda e, k=k: e.tensor_scalar(mn[:, :, 2 * k], mx[:, :, k], -1.0, None, ALU.mult), a, b_)
                    hs.append(DVE.do(lambda e, k=k: e.scalar_tensor_tensor(mn[:, :, 2 * k + 1], mx[:, :, k], -1.0, mn[:, :, 2 * k].bitcast(F32), ALU.mult, ALU.subtract), c))
                bank, i, free = ra.take()
                for qt in range(4):
                    h = PE.do(lambda e, qt=qt: e.transpose(ps[0:16, bank, 128 * qt:128 * qt + 128],
                                                           mn[:, 4 * qt:4 * qt + 4, :].bitcast(F32), ident[:]), *hs, *free, mark=(qt == 3))
                mdone[("mn", G)] = h
                h = DVE.do(lambda e: e.tensor_copy(mrow[:], ps[0:16, bank, :]), h, mdone.get(("row", G - 1)))
                ra.read_by(i, h)
                for j in range(4):
                    mdone[G] = SP.dma(s_m2[s], lambda e, j=j: e.dma_start(Qst[s][96:100, j, :].bitcast(F32), mrow[4 * j:4 * j + 4, :].bitcast(F32)), h, *qst_free[s])
                mdone[("row", G)] = mdone[G]
            return units, rows_of_m

        p_free = [[] for _ in range(3)]
        npt = 0
        o_free = []
        units, rows = max_units(0)
        for u in units:
            u()
        rows()
        a_free = []

        for G in range(NG):
            b, g, s = G // 4, G % 4, G % 2
            if G + 1 < NG:
                units, rows = max_units(G + 1)
            else:
                units, rows = [], None
            pslot = {}
            hexp = {}

            def scores(kt):
                global_p = npt % 3
                pslot[kt] = global_p
                m = 128 if kt < 12 else 65
                hexp[kt] = []
                for pr in range(2):
                    bank, i, free = rb.take()
                    for jj in range(2):
                        j = 2 * pr + jj
                        h = PE.do(lambda e, j=j, jj=jj: e.matmul(ps[:m, bank + jj, :], Kst[s][0:100, j, 128 * kt:128 * kt + m], Qst[s][0:100, j, :],
                                                                 start=True, stop=True), h_k[G], h_q[G], h_indk, mdone[G], *free, mark=(jj == 1))
                    h = ACTQ.do(lambda e, pr=pr: e.activation(P[global_p][:m, 2 * pr:2 * pr + 2, :], ps[:m, bank:bank + 2, :], ACT.Exp, scale=SCALE),
                                h, *p_free[global_p])
                    rb.read_by(i, h)
                    hexp[kt].append(h)
                return h

            def weighted(kt, p0, p1_, first, last):
                pt = P[pslot[kt]]
                for bank in (6, 7):
                    for j in range(4):
                        w = Vg[s][p0:p1_, kt, 32 * j:32 * j + 32] if bank == 6 else ones[p0:p1_, :]
                        h = PE.do(lambda e, bank=bank, j=j, w=w: e.matmul(ps[32 * j:32 * j + 32, bank, :], w, pt[p0:p1_, j, :], start=first, stop=last,
                                                                          tile_position=(p0, 32 * j)),
                                  h_v[G], h_ones, *hexp[kt], *(o_free if first else []), mark=(bank == 7 and j == 3))
                p_free[pslot[kt]] = [h]
                return h

            nu = 0
            for kt in range(NKT + 1):
                if kt < NKT:
                    scores(kt)
                    npt += 1
                    if kt == NKT - 1:
                        kst_last = (PE.sem, PE.n)
                for _ in range(8):
                    if nu < len(units):
                        units[nu]()
                        nu += 1
                        if nu == len(units):
                            rows()
                if 1 <= kt <= 10:
                    weighted(kt - 1, 0, 128, kt == 1, False)
                if kt == 11:
                    h = weighted(10, 0, 64, False, True)
                    h1 = DVE.do(lambda e: e.reciprocal(rt[:], ps[:, 7, :]), h)
                    h2 = DVE.do(lambda e: e.tensor_tensor(ot[:], ps[:, 6, :], rt[:], ALU.mult), h1)
                    o_free = [h2]
                if kt == 12:
                    weighted(10, 64, 128, True, False)
                    weighted(11, 0, 128, False, False)
            h = weighted(12, 0, 65, False, True)
            vg_free[s] = [h]
            kst_free[s] = [kst_last]
            qst_free[s] = [kst_last]
            h1 = DVE.do(lambda e: e.reciprocal(rt[:], ps[:, 7, :]), h, h2)
            h3 = DVE.do(lambda e: e.tensor_tensor(oi[:], ps[:, 6, :], rt[:], ALU.mult), h1)
            o_free = [h3]
            h4 = DVE.do(lambda e: e.tensor_tensor(oi[:], oi[:], ot[:], ALU.add), h3)
            h5 = DVE.do(lambda e: e.tensor_copy(aTh[:, g, :], oi[:]), h4, *a_free)
            h6 = DVE.do(lambda e: e.tensor_sub(aTl[:, g, :], oi[:], aTh[:, g, :].bitcast(F32)), h5)
            if G + 2 < NG:
                load_group(G + 2)
            if g == 3:
                a_free = []
                for t in range(4):
                    bank, i, free = ra.take()
                    for kk in range(4):
                        h = three(ps[:, bank, :], aTh[:, kk, 128 * t:128 * t + 128], aTl[:, kk, 128 * t:128 * t + 128],
                                  Woh[:, kk, :], Wol[:, kk, :], kk == 0, kk == 3, h6, h_wos, *free)
                    k = 4 * b + t
                    d = DVE.do(lambda e, k=k, bank=bank: e.scalar_tensor_tensor(acc[:, k, :], ps[:, bank, :], tg[:, 0:1], acc[:, k, :], ALU.mult, ALU.add), h, h_xb[k])
                    ra.read_by(i, d)
                a_free = [h]
        p2.close()
        barrier()

        p3 = ExitStack()
        xTh = sb(p3, "xTh", [128, 4, 2048], F32R)
        xTl = sb(p3, "xTl", [128, 4, 2048], F32R)
        gur = [sb(p3, f"gur{i}", [128, 4, 512], F32) for i in range(1)]
        dnr = [sb(p3, f"dnr{i}", [128, 2, 512], F32) for i in range(1)]
        guh = [sb(p3, f"guh{i}", [128, 4, 512], F32R) for i in range(2)]
        gul = [sb(p3, f"gul{i}", [128, 4, 512], F32R) for i in range(2)]
        dnh = [sb(p3, f"dnh{i}", [128, 2, 512], F32R) for i in range(2)]
        dnl = [sb(p3, f"dnl{i}", [128, 2, 512], F32R) for i in range(2)]
        ah = [sb(p3, f"ah{i}", [128, 2, 512], F32R) for i in range(2)]
        al = [sb(p3, f"al{i}", [128, 2, 512], F32R) for i in range(2)]
        sg = sb(p3, "sg", [128, 2, 512], F32)
        af = sb(p3, "af", [128, 2, 512], F32)
        xn3 = sb(p3, "xn3", [128, 2, D], F32)
        gtr = sb(p3, "gtr", [128, 4, NE], F32)
        gth = sb(p3, "gth", [128, 4, NE], F32R)
        gtl = sb(p3, "gtl", [128, 4, NE], F32R)
        iot = sb(p3, "iot", [128, NE], F32)
        cmb = sb(p3, "cmb", [128, 16, NE], F32)
        st3 = sb(p3, "st3", [128, 16, 12], F32)
        lg = sb(p3, "lg", [128, 16, NE], F32)
        lm = sb(p3, "lm", [128, 16, NE], F32)
        li = sb(p3, "li", [128, 16, NE], U32)
        wt = sb(p3, "wt", [128, 16, 8], F32)

        s_c3, s_gu, s_out = slot("s_c3"), slot("s_gu"), slot("s_out")
        SP.dma(s_c3, lambda e: e.dma_start(iot[:], ap["iota8"]))
        h_gt = SP.dma(s_c3, lambda e: e.dma_start(gtr[:], ap["w_gate"].rearrange("(k p) n -> p k n", p=128)))
        a = ACTQ.do(lambda e: e.activation(gth[:], gtr[:], ACT.Copy), h_gt)
        h_gts = DVE.do(lambda e: e.tensor_sub(gtl[:], gtr[:], gth[:].bitcast(F32)), a)

        NX = 12
        raw3_free = []
        wx_free = [[], []]
        h_wx = {}

        def load_expert(x):
            nonlocal raw3_free
            s = x % 2
            if x < NE:
                h = SP.dma(s_gu, lambda e: e.dma_start(gur[0][:], ap["w_gate_up"][x].rearrange("(k p) f -> p k f", p=128)), *raw3_free)
                h = SP.dma(s_gu, lambda e: e.dma_start(dnr[0][:], ap["w_down"][x].rearrange("(k p) h -> p k h", p=128)))
            else:
                y = x - NE
                w = ap["w_sh_gate_up"].rearrange("(k p) f -> p k f", p=128)
                SP.dma(s_gu, lambda e: e.dma_start(gur[0][:, :, 0:256], w[:, :, 256 * y:256 * y + 256]), *raw3_free)
                SP.dma(s_gu, lambda e: e.dma_start(gur[0][:, :, 256:512], w[:, :, 1024 + 256 * y:1280 + 256 * y]))
                h = SP.dma(s_gu, lambda e: e.dma_start(dnr[0][:], ap["w_sh_down"][256 * y:256 * y + 256, :].rearrange("(k p) h -> p k h", p=128)))
            a = ACTQ.do(lambda e: e.activation(guh[s][:], gur[0][:], ACT.Copy), h, *wx_free[s])
            b_ = ACTQ.do(lambda e: e.activation(dnh[s][:], dnr[0][:], ACT.Copy), h)
            c = POOL.do(lambda e: e.tensor_tensor(gul[s][:], gur[0][:], guh[s][:].bitcast(F32), ALU.subtract), a, *wx_free[s])
            d = POOL.do(lambda e: e.tensor_tensor(dnl[s][:], dnr[0][:], dnh[s][:].bitcast(F32), ALU.subtract), b_)
            raw3_free = [a, b_, c, d]
            h_wx[x] = [a, b_, c, d]

        load_expert(0)
        tr3 = Banks([0, 1])
        h_xt, xn3_free, h_cmb = [], [None] * 2, []
        for k in range(16):
            xs = k % 2
            a = DVE.do(lambda e, k=k: e.bn_stats(st3[:, k, 0:6], acc[:, k, :]))
            a = DVE.do(lambda e, k=k: e.bn_aggr(st3[:, k, 6:8], st3[:, k, 0:6]), a)
            a = DVE.do(lambda e, k=k: e.tensor_scalar(st3[:, k, 8:9], st3[:, k, 7:8], 1e-5, None, ALU.add), a)
            c = ACTQ.do(lambda e, k=k: e.activation(st3[:, k, 9:10], st3[:, k, 8:9], ACT.Sqrt), a)
            d = DVE.do(lambda e, k=k: e.reciprocal(st3[:, k, 10:11], st3[:, k, 9:10]), c)
            d = DVE.do(lambda e, k=k, xs=xs: e.tensor_scalar(xn3[:, xs, :], acc[:, k, :], st3[:, k, 6:7], st3[:, k, 10:11], ALU.subtract, ALU.mult), d, xn3_free[xs])
            bank, i, free = tr3.take()
            for g in range(4):
                h = PE.do(lambda e, g=g, xs=xs, bank=bank: e.transpose(ps[:, bank, 128 * g:128 * g + 128], xn3[:, xs, 128 * g:128 * g + 128], ident[:]), d, *free, mark=(g == 3))
            xn3_free[xs] = h
            v = ps[:, bank, :].rearrange("p (g s) -> p g s", g=4)
            hi, lo = xTh[:, :, 128 * k:128 * k + 128], xTl[:, :, 128 * k:128 * k + 128]
            a = ACTQ.do(lambda e, hi=hi, v=v: e.activation(hi, v, ACT.Copy), h)
            d = DVE.do(lambda e, hi=hi, lo=lo, v=v: e.tensor_sub(lo, v, hi.bitcast(F32)), a)
            tr3.read_by(i, a)
            tr3.read_by(i, d)
            h_xt.append((a, d))
        lg3 = Banks([2, 3])
        for k in range(16):
            bank, i, free = lg3.take()
            for kk in range(4):
                h = three(ps[:, bank, 0:NE], xTh[:, kk, 128 * k:128 * k + 128], xTl[:, kk, 128 * k:128 * k + 128],
                          gth[:, kk, :], gtl[:, kk, :], kk == 0, kk == 3, *h_xt[k], h_gts, *free)
            d = DVE.do(lambda e, k=k, bank=bank: e.tensor_copy(lg[:, k, :], ps[:, bank, 0:NE]), h)
            lg3.read_by(i, d)
            d = DVE.do(lambda e, k=k: e.max(lm[:, k, :], lg[:, k, :]), d)
            d = DVE.do(lambda e, k=k: e.max_index(li[:, k, :], lm[:, k, :], lg[:, k, :]), d)
        h_li = d
        a = DVE.do(lambda e: e.tensor_sub(wt[:, :, 0], lm[:, :, 1], lm[:, :, 0]), h_li)
        c = ACTQ.do(lambda e: e.activation(wt[:, :, 1], wt[:, :, 0], ACT.Exp), a)
        a = DVE.do(lambda e: e.tensor_scalar(wt[:, :, 2], wt[:, :, 1], 1.0, None, ALU.add), c)
        a = DVE.do(lambda e: e.reciprocal(wt[:, :, 3], wt[:, :, 2]), a)
        a = DVE.do(lambda e: e.tensor_scalar(wt[:, :, 4], wt[:, :, 3], tg[:, 1:2], None, ALU.mult), a)
        a = DVE.do(lambda e: e.tensor_tensor(wt[:, :, 5], wt[:, :, 4], wt[:, :, 1], ALU.mult), a)
        a = DVE.do(lambda e: e.tensor_copy(wt[:, :, 6:8], li[:, :, 0:2]), a, h_li)
        for k in range(16):
            d = DVE.do(lambda e, k=k: e.tensor_scalar(lg[:, k, :], iot[:], wt[:, k, 7:8], wt[:, k, 5:6], ALU.is_equal, ALU.mult), a, h_gt)
            d = DVE.do(lambda e, k=k: e.tensor_scalar(cmb[:, k, :], iot[:], wt[:, k, 6:7], wt[:, k, 4:5], ALU.is_equal, ALU.mult), d)
            d = DVE.do(lambda e, k=k: e.tensor_tensor(cmb[:, k, :], cmb[:, k, :], lg[:, k, :], ALU.add), d)
        h_cmb = d

        up3, dn3 = Banks([0, 1, 2, 3, 4]), Banks([5, 6, 7])
        first_waits = [h for pair in h_xt for h in pair] + [h_cmb]
        a_free3 = [[], []]
        sg_free, af_free = [None] * 2, [[] for _ in range(2)]
        pend = None
        acc_last = [None] * 16
        nstep = 0

        def down(x, tb, s, hact):
            w = x % 2
            for t in range(4):
                bank, i, free = dn3.take()
                k = 4 * tb + t
                for kk in range(2):
                    h = three(ps[:, bank, :], ah[s][:, kk, 128 * t:128 * t + 128], al[s][:, kk, 128 * t:128 * t + 128],
                              dnh[w][:, kk, :], dnl[w][:, kk, :], kk == 0, kk == 1, *hact, *h_wx[x], *free)
                sc = cmb[:, k, x:x + 1] if x < NE else tg[:, 1:2]
                d = DVE.do(lambda e, k=k, bank=bank, sc=sc: e.scalar_tensor_tensor(acc[:, k, :], ps[:, bank, :], sc, acc[:, k, :], ALU.mult, ALU.add), h, acc_last[k])
                dn3.read_by(i, d)
                acc_last[k] = d
            a_free3[s] = [h]
            if tb == 3:
                wx_free[w] = [h]
                if x + 2 < NX:
                    load_expert(x + 2)
            if x == NX - 1:
                for t in range(4):
                    k = 4 * tb + t
                    SP.dma(s_out, lambda e, k=k: e.dma_start(ap["out"].rearrange("b (t p) d -> p (b t) d", p=128)[:, k, :], acc[:, k, :]), acc_last[k])

        load_expert(1)
        for x in range(NX):
            w = x % 2
            for tb in range(4):
                s = nstep % 2
                nstep += 1
                hact = []
                for f in range(2):
                    got = []
                    for half in range(2):
                        bank, i, free = up3.take()
                        c0 = 256 * half + 128 * f
                        for kk in range(4):
                            h = three(ps[:, bank, :], guh[w][:, kk, c0:c0 + 128], gul[w][:, kk, c0:c0 + 128],
                                      xTh[:, kk, 512 * tb:512 * tb + 512], xTl[:, kk, 512 * tb:512 * tb + 512], kk == 0, kk == 3,
                                      *h_wx[x], *first_waits, *free)
                        got.append((bank, i, h))
                    (bg, ig, hg), (bu, iu, hu) = got
                    a = ACTQ.do(lambda e, f=f, bg=bg: e.activation(sg[:, f, :], ps[:, bg, :], ACT.Silu), hg, sg_free[f])
                    up3.read_by(ig, a)
                    d = DVE.do(lambda e, f=f, bu=bu: e.tensor_tensor(af[:, f, :], sg[:, f, :], ps[:, bu, :], ALU.mult), a, hu, *af_free[f])
                    up3.read_by(iu, d)
                    sg_free[f] = d
                    c = ACTQ.do(lambda e, f=f, s=s: e.activation(ah[s][:, f, :], af[:, f, :], ACT.Copy), d, *a_free3[s])
                    g_ = DVE.do(lambda e, f=f, s=s: e.tensor_sub(al[s][:, f, :], af[:, f, :], ah[s][:, f, :].bitcast(F32)), c, *a_free3[s])
                    af_free[f] = [g_]
                    hact += [c, g_]
                if pend:
                    down(*pend)
                pend = (x, tb, s, hact)
        down(*pend)
        SP.wait((s_out.sem, s_out.n))
        for s in slots:
            SP.wait((s.sem, s.n))

        p3.close()


def kernel(**inputs):
    import concourse.bacc as _bacc
    from concourse.bass_utils import run_bass_kernel_spmd as _run

    def X(n):
        return np.asarray(inputs[n])

    c = X("ctx_2048")
    ctxT = np.ascontiguousarray(np.concatenate([c[:, NIMG:], c[:, :NIMG]], axis=1).transpose(0, 2, 1))
    ind = np.zeros((4, NKP), np.float32)
    ind[0:2, :NTXT] = 1.0
    ind[2:4, NTXT:] = 1.0
    arrays = {
        "x": X("x"), "ctxT": ctxT, "g_xattn": X("g_xattn"), "g_ffn": X("g_ffn"),
        "ident": np.eye(128, dtype=np.float32), "ind": ind,
        "iota8": np.ascontiguousarray(np.broadcast_to(np.arange(8, dtype=np.float32), (128, 8))),
        "w_gate": X("L0_ffn_w_gate"), "w_gate_up": X("L0_ffn_w_gate_up"), "w_down": X("L0_ffn_w_down"),
        "w_sh_gate_up": X("L0_ffn_w_sh_gate_up"), "w_sh_down": X("L0_ffn_w_sh_down"),
    }
    for n in ("q_b", "k_b", "v_b", "k_img_b", "v_img_b", "o_b", "norm_q_w", "norm_k_w", "norm_k_img_w"):
        arrays[n] = X("L0_xattn_" + n)
    for n in ("q_w", "k_w", "v_w", "k_img_w", "v_img_w", "o_w"):
        arrays[n + "T"] = np.ascontiguousarray(X("L0_xattn_" + n).T)

    nc = _bacc.Bacc("TRN2", target_bir_lowering=False, num_devices=1)
    ins, ap = {}, {}
    for name, a in arrays.items():
        a = np.ascontiguousarray(a)
        ins["in_" + name] = a
        ap[name] = nc.dram_tensor("in_" + name, a.shape, mybir.dt.from_np(a.dtype), kind="ExternalInput").ap()
    ap["out"] = nc.dram_tensor("out_0", (NB, LQ, D), F32, kind="ExternalOutput").ap()
    flamingo_program(nc, ap)
    r = _run(nc, [ins], core_ids=[0])
    return r.results[0]["out_0"]
```

```python
import numpy as np
from contextlib import ExitStack

import concourse.bass as bass
from concourse import mybir

F32 = mybir.dt.float32
F32R = mybir.dt.float32r
U32 = mybir.dt.uint32
ACT = mybir.ActivationFunctionType
ALU = mybir.AluOpType
AX = mybir.AxisListType

NB = 4
D = 512
LQ = 512
NTXT, NIMG = 1344, 257
NK = NTXT + NIMG
NKP = NK + 1
NKT = 13
SCALE = 1.0 / float(np.sqrt(np.float32(32.0)))
NE = 8


class Queue:

    def __init__(self, eng, sem):
        self.eng, self.sem, self.n, self.seen = eng, sem, 0, {}

    def wait(self, *handles):
        for h in handles:
            if h is not None and self.seen.get(h[0].name, 0) < h[1]:
                self.eng.wait_ge(*h)
                self.seen[h[0].name] = h[1]

    def do(self, fn, *waits, mark=True):
        self.wait(*waits)
        ins = fn(self.eng)
        if mark:
            ins.then_inc(self.sem, 1)
            self.n += 1
            return (self.sem, self.n)
        return None

    def dma(self, slot, fn, *waits):
        self.wait(*waits)
        fn(self.eng).then_inc(slot.sem, 16)
        slot.n += 16
        return (slot.sem, slot.n)


class Slot:

    def __init__(self, sem):
        self.sem, self.n = sem, 0


class Banks:

    def __init__(self, banks):
        self.banks, self.at, self.readers = banks, 0, [[] for _ in banks]

    def take(self):
        i = self.at % len(self.banks)
        self.at += 1
        r, self.readers[i] = self.readers[i], []
        return self.banks[i], i, r

    def read_by(self, i, handle):
        self.readers[i].append(handle)


def flamingo_program(nc, ap):
    ctx = ExitStack()
    with ctx:
        def sem(name):
            return ctx.enter_context(nc.semaphore(name))

        PE, DVE, ACTQ, POOL, SP = (Queue(e, sem(n)) for e, n in (
            (nc.tensor, "c_pe"), (nc.vector, "c_dve"), (nc.scalar, "c_act"), (nc.gpsimd, "c_pool"), (nc.sync, "c_sp")))
        slots = []

        def slot(name):
            slots.append(Slot(sem(name)))
            return slots[-1]

        def sb(stack, name, shape, dt):
            return stack.enter_context(nc.sbuf_tensor(name, shape, dt))

        ps = ctx.enter_context(nc.psum_tensor("ps", [128, 8, 512], F32))

        KHd = nc.dram_tensor("KHd", (NB, D, NKP), F32).ap()
        KLd = nc.dram_tensor("KLd", (NB, D, NKP), F32).ap()
        Vd = nc.dram_tensor("Vd", (NB, NK, D), F32).ap()
        QHd = nc.dram_tensor("QHd", (NB, D, LQ), F32).ap()
        QLd = nc.dram_tensor("QLd", (NB, D, LQ), F32).ap()

        def barrier():
            h = [(q.sem, q.n) for q in (PE, DVE, ACTQ, POOL) if q.n] + [(s.sem, s.n) for s in slots if s.n]
            for q in (PE, DVE, ACTQ, POOL, SP):
                q.wait(*h)

        def three(out, ah, al, bh, bl, first, last, *waits):
            PE.do(lambda e: e.matmul(out, ah, bh, start=first, stop=False), *waits, mark=False)
            PE.do(lambda e: e.matmul(out, ah, bl, start=False, stop=False), mark=False)
            return PE.do(lambda e: e.matmul(out, al, bh, start=False, stop=last), mark=last)

        ident = sb(ctx, "ident", [128, 128], F32)
        acc = sb(ctx, "acc", [128, 16, D], F32)
        tg = sb(ctx, "tg", [128, 2], F32)
        gin = sb(ctx, "gin", [128, 2], F32)
        s_c = slot("s_c")
        h_id = SP.dma(s_c, lambda e: e.dma_start(ident[:], ap["ident"]))
        SP.dma(s_c, lambda e: e.dma_start(gin[:, 0:1], ap["g_xattn"].partition_broadcast(128)))
        h_g = SP.dma(s_c, lambda e: e.dma_start(gin[:, 1:2], ap["g_ffn"].partition_broadcast(128)))
        h_id = h_g
        h_tg = ACTQ.do(lambda e: e.activation(tg[:], gin[:], ACT.Tanh), h_g)

        p1 = ExitStack()
        bias = sb(p1, "bias", [128, 8, D], F32)
        QB, QNW, KB, KNW, VB, KIB, KINW, VIB = range(8)
        Wh = sb(p1, "Wh", [128, 5, 4, D], F32R)
        Wl = sb(p1, "Wl", [128, 5, 4, D], F32R)
        wraw = sb(p1, "wraw", [128, 4, D], F32)
        raw = sb(p1, "raw", [128, 2, 4, 256], F32)
        ch = sb(p1, "ch", [128, 2, 4, 256], F32R)
        cl = sb(p1, "cl", [128, 2, 4, 256], F32R)
        kf = sb(p1, "kf", [128, 3, D], F32)
        vf = sb(p1, "vf", [128, 3, D], F32)
        junk = sb(p1, "junk", [128, D], F32)
        sth = sb(p1, "sth", [128, 2, 4, 258], F32R)
        stl = sb(p1, "stl", [128, 2, 4, 258], F32R)
        xn = sb(p1, "xn", [128, 2, D], F32)
        st = sb(p1, "st", [128, 8, 8], F32)
        bst = sb(p1, "bst", [128, 2, 6], F32)
        mv = sb(p1, "mv", [128, 2, 2], F32)

        s_b, s_x, s_x0, s_w = slot("s_b"), slot("s_x"), slot("s_x0"), slot("s_w")
        s_raw = [slot(f"s_raw{i}") for i in range(2)]
        s_st = [slot(f"s_st{i}") for i in range(2)]
        s_v = [slot(f"s_v{i}") for i in range(3)]

        xv = ap["x"].rearrange("b (t p) d -> p (b t) d", p=128)
        h_x = [SP.dma(s_x0, lambda e: e.dma_start(acc[:, 0:4, :], xv[:, 0:4, :]))]
        WQ, WK, WV, WKI, WVI = range(5)
        wsplit, wfree = {}, None

        def load_w(w, name):
            nonlocal wfree
            h = SP.dma(s_w, lambda e: e.dma_start(wraw[:], ap[name].rearrange("(k p) o -> p k o", p=128)), wfree)
            hh = ACTQ.do(lambda e: e.activation(Wh[:, w], wraw[:], ACT.Copy), h)
            hl = DVE.do(lambda e: e.tensor_sub(Wl[:, w], wraw[:], Wh[:, w].bitcast(F32)), h, hh)
            wfree = hl
            wsplit[w] = (hh, hl)

        load_w(WQ, "q_wT")
        names = ["q_b", "norm_q_w", "k_b", "norm_k_w", "v_b", "k_img_b", "norm_k_img_w", "v_img_b"]
        for i, n in enumerate(names):
            h_bias = SP.dma(s_b, lambda e: e.dma_start(bias[:, i, :], ap[n].partition_broadcast(128)))
        h_x += [SP.dma(s_x, lambda e: e.dma_start(acc[:, 4:16, :], xv[:, 4:16, :]))] * 3
        later_w = [(WK, "k_wT"), (WV, "v_wT"), (WKI, "k_img_wT"), (WVI, "v_img_wT")]

        mm, tr = Banks(range(0, 6)), Banks(range(6, 8))
        nst = 0
        st_last = [None] * 8

        def rms(src, rows, row_wait, nw):
            nonlocal nst
            r = nst % 8
            nst += 1
            a = ACTQ.do(lambda e: e.activation(junk[:rows], src, ACT.Square, accum_out=st[:rows, r, 0:1]),
                        row_wait, st_last[r], (ACTQ.sem, ACTQ.n) if ACTQ.n else None)
            b_ = DVE.do(lambda e: e.tensor_scalar(st[:rows, r, 1:2], st[:rows, r, 0:1], 1.0 / D, 1e-6, ALU.mult, ALU.add), a)
            c = ACTQ.do(lambda e: e.activation(st[:rows, r, 2:3], st[:rows, r, 1:2], ACT.Sqrt), b_)
            d = DVE.do(lambda e: e.reciprocal(st[:rows, r, 3:4], st[:rows, r, 2:3]), c)
            h = DVE.do(lambda e: e.scalar_tensor_tensor(src, src, st[:rows, r, 3:4], bias[:rows, nw, :], ALU.mult, ALU.mult), d)
            st_last[r] = h
            return h

        kf_free, vf_free = [None] * 3, [None] * 3
        st_free = [[] for _ in range(2)]
        nkf = nvf = 0

        def transposed(src, rows, src_wait, hi, lo, dst_waits, extra=False):
            bank, i, free = tr.take()
            for g in range(4):
                h = PE.do(lambda e, g=g: e.transpose(ps[:, bank, g * 128:g * 128 + rows], src[:, g * 128:g * 128 + 128], ident[:rows, :rows]),
                          src_wait, h_id, *free, mark=(g == 3))
            v = ps[:, bank, :].rearrange("p (g s) -> p g s", g=4)[:, :, 0:rows]
            a = ACTQ.do(lambda e: e.activation(hi, v, ACT.Copy), h, *dst_waits)
            d = DVE.do(lambda e: e.tensor_sub(lo, v, hi.bitcast(F32)), a, *dst_waits)
            tr.read_by(i, a)
            tr.read_by(i, d)
            return a, d, h

        xn_free = [None] * 2
        ch_free = [None] * 2
        q_pending = []

        q_done = []

        def finish_q(b, t, slot3, hnorm):
            s, c0 = (t // 2) % 2, 128 * (t % 2)
            a, d, ht = transposed(kf[:, slot3, :], 128, hnorm, sth[:, s, :, c0:c0 + 128], stl[:, s, :, c0:c0 + 128], st_free[s])
            kf_free[slot3] = ht
            q_done.extend([a, d])
            if t % 2:
                for src, dst in ((sth, QHd), (stl, QLd)):
                    st_free[s] = [SP.dma(s_st[s], lambda e, src=src, dst=dst: e.dma_start(
                        dst[b].rearrange("(k p) s -> p k s", p=128)[:, :, 256 * s:256 * s + 256], src[:, s, :, 0:256].bitcast(F32)), *q_done)]
                q_done.clear()

        def normed_x(k):
            nonlocal nst
            xs = k % 2
            a = DVE.do(lambda e: e.bn_stats(bst[:, xs, :], acc[:, k, :]), h_x[k // 4])
            a = DVE.do(lambda e: e.bn_aggr(mv[:, xs, :], bst[:, xs, :]), a)
            r = nst % 8
            nst += 1
            a = DVE.do(lambda e: e.tensor_scalar(st[:, r, 1:2], mv[:, xs, 1:2], 1e-5, None, ALU.add), a, st_last[r])
            c = ACTQ.do(lambda e: e.activation(st[:, r, 2:3], st[:, r, 1:2], ACT.Sqrt), a)
            d = DVE.do(lambda e: e.reciprocal(st[:, r, 3:4], st[:, r, 2:3]), c)
            d = DVE.do(lambda e: e.tensor_scalar(xn[:, xs, :], acc[:, k, :], mv[:, xs, 0:1], st[:, r, 3:4], ALU.subtract, ALU.mult), d, xn_free[xs])
            st_last[r] = d
            a, d, ht = transposed(xn[:, xs, :], 128, d, ch[:, xs, :, 0:128], cl[:, xs, :, 0:128], [ch_free[xs]])
            xn_free[xs] = ht
            return a, d

        h_xn = {0: normed_x(0)}
        for k in range(16):
            xs = k % 2
            if k + 1 < 16:
                h_xn[k + 1] = normed_x(k + 1)
            bank, i, free = mm.take()
            for kk in range(4):
                hq = three(ps[:, bank, :], ch[:, xs, kk, 0:128], cl[:, xs, kk, 0:128], Wh[:, WQ, kk, :], Wl[:, WQ, kk, :],
                           kk == 0, kk == 3, *h_xn[k], *wsplit[WQ], *free)
            ch_free[xs] = hq
            s3 = nkf % 3
            nkf += 1
            h = DVE.do(lambda e: e.tensor_tensor(kf[:, s3, :], ps[:, bank, :], bias[:, QB, :], ALU.add), hq, h_bias, kf_free[s3])
            mm.read_by(i, h)
            h = rms(kf[:, s3, :], 128, h, QNW)
            if q_pending:
                finish_q(*q_pending.pop())
            q_pending.append((k // 4, k % 4, s3, h))
            if k in (2, 5, 8, 11):
                load_w(*later_w.pop(0))
        finish_q(*q_pending.pop())

        raw_free = [[] for _ in range(2)]
        ctf = ap["ctxT"]
        k_pending = []
        nchunk = 0

        def finish_k(b, c, j, rows, s, s3, hnorm, last, width):
            c0 = 128 * j
            a, d, ht = transposed(kf[:rows, s3, :], rows, hnorm, sth[:, s, :, c0:c0 + rows], stl[:, s, :, c0:c0 + rows], st_free[s])
            kf_free[s3] = ht
            k_done.extend([a, d])
            if c == 6:
                for q, dst in ((ACTQ, sth), (DVE, stl)):
                    if q is ACTQ:
                        k_done.append(q.do(lambda e, dst=dst: e.activation(dst[:, s, :, rows:rows + 1], dst[:, s, :, rows - 1:rows].bitcast(F32), ACT.Copy), a))
                    else:
                        k_done.append(q.do(lambda e, dst=dst: e.tensor_copy(dst[:, s, :, rows:rows + 1], dst[:, s, :, rows - 1:rows].bitcast(F32)), d))
            if last:
                for src, dst in ((sth, KHd), (stl, KLd)):
                    st_free[s] = [SP.dma(s_st[s], lambda e, src=src, dst=dst: e.dma_start(
                        dst[b].rearrange("(k p) s -> p k s", p=128)[:, :, 256 * c:256 * c + width],
                        src[:, s, :, 0:width].bitcast(F32)), *k_done)]
                k_done.clear()

        k_done = []
        chunks = [(b, c) for b in range(NB) for c in range(7)]
        h_raw, h_split = {}, {}

        def load_chunk(n):
            (b, c), s = chunks[n], n % 2
            w = 256 if c < 6 else 65
            h_raw[n] = SP.dma(s_raw[s], lambda e: e.dma_start(
                raw[:, s, :, 0:w], ctf[b].rearrange("(k p) s -> p k s", p=128)[:, :, 256 * c:256 * c + w]), *raw_free[s])

        def split_chunk(n):
            (b, c), s = chunks[n], n % 2
            w = 256 if c < 6 else 65
            hh = ACTQ.do(lambda e: e.activation(ch[:, s, :, 0:w], raw[:, s, :, 0:w], ACT.Copy), h_raw[n], ch_free[s])
            hl = POOL.do(lambda e: e.tensor_tensor(cl[:, s, :, 0:w], raw[:, s, :, 0:w], ch[:, s, :, 0:w].bitcast(F32), ALU.subtract), h_raw[n], hh, ch_free[s])
            raw_free[s] = [hh, hl]
            h_split[n] = (hh, hl)

        load_chunk(0)
        load_chunk(1)
        split_chunk(0)
        for b in range(NB):
            for c in range(7):
                n = 256 if c < 6 else 65
                s = nchunk % 2
                hh, hl = h_split[nchunk]
                if nchunk + 1 < len(chunks):
                    split_chunk(nchunk + 1)
                if nchunk + 2 < len(chunks):
                    load_chunk(nchunk + 2)
                nchunk += 1
                for j in range(2 if c < 6 else 1):
                    rows = 128 if c < 6 else 65
                    t = 2 * c + j
                    if t < 10:
                        parts = [(0, 128, WK, WV, KB, KNW, VB)]
                    elif t == 10:
                        parts = [(0, 64, WK, WV, KB, KNW, VB), (64, 128, WKI, WVI, KIB, KINW, VIB)]
                    else:
                        parts = [(0, rows, WKI, WVI, KIB, KINW, VIB)]
                    s3 = nkf % 3
                    nkf += 1
                    hk = []
                    for p0, p1_, wk, wv, kb, knw, vb in parts:
                        bank, i, free = mm.take()
                        for kk in range(4):
                            hm = three(ps[:rows, bank, :], ch[:, s, kk, 128 * j:128 * j + rows], cl[:, s, kk, 128 * j:128 * j + rows],
                                       Wh[:, wk, kk, :], Wl[:, wk, kk, :], kk == 0, kk == 3, hh, hl, *wsplit[wk], *free)
                        h = DVE.do(lambda e, s3=s3, bank=bank, p0=p0, p1_=p1_, kb=kb: e.tensor_tensor(
                            kf[p0:p1_, s3, :], ps[p0:p1_, bank, :], bias[p0:p1_, kb, :], ALU.add), hm, kf_free[s3])
                        mm.read_by(i, h)
                        hk.append(h)
                    if len(parts) == 2:
                        r = nst % 8
                        nst += 1
                        a = ACTQ.do(lambda e, s3=s3, r=r: e.activation(junk[:], kf[:, s3, :], ACT.Square, accum_out=st[:, r, 0:1]), hk[-1], st_last[r], (ACTQ.sem, ACTQ.n))
                        a = DVE.do(lambda e, r=r: e.tensor_scalar(st[:, r, 1:2], st[:, r, 0:1], 1.0 / D, 1e-6, ALU.mult, ALU.add), a)
                        a = ACTQ.do(lambda e, r=r: e.activation(st[:, r, 2:3], st[:, r, 1:2], ACT.Sqrt), a)
                        d = DVE.do(lambda e, r=r: e.reciprocal(st[:, r, 3:4], st[:, r, 2:3]), a)
                        for p0, p1_, nw in ((0, 64, KNW), (64, 128, KINW)):
                            hn = DVE.do(lambda e, s3=s3, r=r, p0=p0, p1_=p1_, nw=nw: e.scalar_tensor_tensor(
                                kf[p0:p1_, s3, :], kf[p0:p1_, s3, :], st[p0:p1_, r, 3:4], bias[p0:p1_, nw, :], ALU.mult, ALU.mult), d)
                        st_last[r] = hn
                    else:
                        hn = rms(kf[:rows, s3, :], rows, hk[-1], parts[0][5])
                    if k_pending:
                        finish_k(*k_pending.pop())
                    sv = nvf % 3
                    nvf += 1
                    for p0, p1_, wk, wv, kb, knw, vb in parts:
                        bank, i, free = mm.take()
                        for kk in range(4):
                            hm = three(ps[:rows, bank, :], ch[:, s, kk, 128 * j:128 * j + rows], cl[:, s, kk, 128 * j:128 * j + rows],
                                       Wh[:, wv, kk, :], Wl[:, wv, kk, :], kk == 0, kk == 3, *wsplit[wv], *free)
                        h = DVE.do(lambda e, sv=sv, bank=bank, p0=p0, p1_=p1_, vb=vb: e.tensor_tensor(
                            vf[p0:p1_, sv, :], ps[p0:p1_, bank, :], bias[p0:p1_, vb, :], ALU.add), hm, vf_free[sv])
                        mm.read_by(i, h)
                    vf_free[sv] = SP.dma(s_v[sv], lambda e, b=b, t=t, rows=rows, sv=sv: e.dma_start(
                        Vd[b, 128 * t:128 * t + rows, :], vf[:rows, sv, :]), h)
                    ch_free[s] = hm
                    k_pending.append((b, c, j, rows, s, s3, hn, j == 1 or c == 6, n if c < 6 else 66))
        finish_k(*k_pending.pop())
        p1.close()
        barrier()

        p2 = ExitStack()
        Kst = [sb(p2, f"Kst{i}", [128, 4, NKP], F32R) for i in range(2)]
        Qst = [sb(p2, f"Qst{i}", [128, 4, LQ], F32R) for i in range(2)]
        Vg = [sb(p2, f"Vg{i}", [128, NKT, 128], F32) for i in range(2)]
        P = [sb(p2, f"P{i}", [128, 4, LQ], F32) for i in range(4)]
        sacc = sb(p2, "sacc", [128, 4, LQ], F32)
        aTh = sb(p2, "aTh", [128, 4, LQ], F32R)
        aTl = sb(p2, "aTl", [128, 4, LQ], F32R)
        Woh = sb(p2, "Woh", [128, 4, D], F32R)
        Wol = sb(p2, "Wol", [128, 4, D], F32R)
        woraw = P[1]
        obb = sb(p2, "obb", [128, D], F32)
        rt = sb(p2, "rt", [128, D], F32)
        ot = sb(p2, "ot", [128, D], F32)
        oi = sb(p2, "oi", [128, D], F32)
        rr = sb(p2, "rr", [128, D], F32)
        pp = sb(p2, "pp", [128, D], F32)
        ones = sb(p2, "ones", [128, 32], F32)
        mp = sb(p2, "mp", [128, 16, 4], F32)
        mx = sb(p2, "mx", [128, 16, 2], F32)
        mn = sb(p2, "mn", [128, 16, 4], F32R)
        mrow = sb(p2, "mrow", [16, LQ], F32R)

        s_k2 = [[slot(f"s_k2{i}{j}") for j in range(2)] for i in range(2)]
        s_q2 = [slot(f"s_q2{i}") for i in range(2)]
        s_v2 = [slot(f"s_v2{i}") for i in range(2)]
        s_m2 = [slot(f"s_m2{i}") for i in range(2)]
        s_c2 = slot("s_c2")

        NG = 4 * NB
        kst_free = [[] for _ in range(2)]
        qst_free = [[] for _ in range(2)]
        vg_free = [[] for _ in range(2)]
        h_k, h_q, h_v = {}, {}, {}

        indf = P[0][96:100].rearrange("p a b -> p (a b)")[:, 0:NKP]
        h_ind = SP.dma(s_c2, lambda e: e.dma_start(indf, ap["ind"]))

        def load_group(G):
            b, g, s = G // 4, G % 4, G % 2
            rows = slice(128 * g, 128 * g + 128)

            def head_rows(d):
                return d[b, rows, :].rearrange("(j p) s -> p j s", p=32)
            for p0, d in ((0, QHd), (32, QLd), (64, QHd)):
                h_q[G] = SP.dma(s_q2[s], lambda e, p0=p0, d=d: e.dma_start(Qst[s][p0:p0 + 32].bitcast(F32), head_rows(d)), *qst_free[s])
            for jp in range(2):
                for p0, d in ((0, KHd), (32, KHd), (64, KLd)):
                    h_k[G, jp] = SP.dma(s_k2[s][jp], lambda e: e.dma_start(
                        Kst[s][p0:p0 + 32, 2 * jp:2 * jp + 2, :].bitcast(F32), head_rows(d)[:, 2 * jp:2 * jp + 2, :]), *kst_free[s])
            SP.dma(s_v2[s], lambda e: e.dma_start(
                Vg[s][:, 0:12, :], Vd[b, 0:1536, rows].rearrange("(t p) d -> p t d", p=128)), *vg_free[s])
            h_v[G] = SP.dma(s_v2[s], lambda e: e.dma_start(Vg[s][0:65, 12, :], Vd[b, 1536:NK, rows]))

        load_group(0)
        h_wo = SP.dma(s_c2, lambda e: e.dma_start(woraw[:], ap["o_wT"].rearrange("(k p) o -> p k o", p=128)))
        h_ob = SP.dma(s_c2, lambda e: e.dma_start(obb[:], ap["o_b"].partition_broadcast(128)))
        h_ind = h_wo = h_ob
        load_group(1)
        h_ones = DVE.do(lambda e: e.memset(ones[:], 1.0))
        hi_ = []
        for s in range(2):
            for j in range(4):
                hi_.append(ACTQ.do(lambda e, s=s, j=j: e.activation(Kst[s][96:100, j, :], indf, ACT.Copy), h_ind))
        h_indk = hi_[-1]
        a = ACTQ.do(lambda e: e.activation(Woh[:], woraw[:], ACT.Copy), h_wo)
        h_wos = DVE.do(lambda e: e.tensor_sub(Wol[:], woraw[:], Woh[:].bitcast(F32)), a)
        h_xb = []
        for k in range(16):
            h_xb.append(DVE.do(lambda e, k=k: e.scalar_tensor_tensor(acc[:, k, :], obb[:], tg[:, 0:1], acc[:, k, :], ALU.mult, ALU.add), h_ob, h_tg))

        ra, rb = Banks([0, 1]), Banks([2, 4])
        CH = [(0, 512), (512, 1024), (1024, NTXT), (NTXT, NKP)]
        mdone = {}

        def max_units(G):
            s = G % 2
            last = {}
            units = []
            for j in range(4):
                for qt in range(4):
                    for c, (c0, c1) in enumerate(CH):
                        def unit(qt=qt, j=j, c=c, c0=c0, c1=c1):
                            bank, i, free = ra.take()
                            h = PE.do(lambda e: e.matmul(ps[:, bank, 0:c1 - c0], Qst[s][0:96, j, 128 * qt:128 * qt + 128],
                                                         Kst[s][0:96, j, c0:c1], start=True, stop=True), h_k[G, j // 2], h_q[G], *free)
                            h = DVE.do(lambda e: e.reduce_max(mp[:, 4 * qt + j, c:c + 1], ps[:, bank, 0:c1 - c0], AX.X), h, last.get("mpfree"))
                            ra.read_by(i, h)
                            last["h"] = h
                            last["pe"] = (PE.sem, PE.n)
                        units.append(unit)

            hs = []

            def negated():
                a = DVE.do(lambda e: e.tensor_reduce(mx[:, :, 0], mp[:, :, 0:3], axis=AX.X, op=ALU.max), last["h"], mdone.get(("mn", G - 1)))
                b_ = DVE.do(lambda e: e.tensor_copy(mx[:, :, 1], mp[:, :, 3]), last["h"])
                for k in range(2):
                    c = DVE.do(lambda e, k=k: e.tensor_scalar(mn[:, :, 2 * k], mx[:, :, k], -1.0, None, ALU.mult), a, b_)
                    hs.append(DVE.do(lambda e, k=k: e.scalar_tensor_tensor(mn[:, :, 2 * k + 1], mx[:, :, k], -1.0, mn[:, :, 2 * k].bitcast(F32), ALU.mult, ALU.subtract), c))

            def rows_of_m():
                bank, i, free = ra.take()
                for qt in range(4):
                    h = PE.do(lambda e, qt=qt: e.transpose(ps[0:16, bank, 128 * qt:128 * qt + 128],
                                                           mn[:, 4 * qt:4 * qt + 4, :].bitcast(F32), ident[:]), *hs, *free, mark=(qt == 3))
                mdone[("mn", G)] = h
                h = DVE.do(lambda e: e.tensor_copy(mrow[:], ps[0:16, bank, :]), h, mdone.get(("row", G - 1)))
                ra.read_by(i, h)
                for j in range(4):
                    mdone[G] = SP.dma(s_m2[s], lambda e, j=j: e.dma_start(Qst[s][96:100, j, :].bitcast(F32), mrow[4 * j:4 * j + 4, :].bitcast(F32)), h, *qst_free[s])
                mdone[("row", G)] = mdone[G]
            return units, negated, rows_of_m

        p_free = [[] for _ in range(4)]
        npt = 0
        o_free = []
        units, negated, rows = max_units(0)
        for u in units:
            u()
        negated()
        rows()
        a_free = []
        sacc_free, ot_free = None, None
        ON_POOL = (0, 1, 2, 4, 5, 7, 8)
        due = []

        def project(b, h6):
            for t in range(4):
                bank, i, free = ra.take()
                for kk in range(4):
                    h = three(ps[:, bank, :], aTh[:, kk, 128 * t:128 * t + 128], aTl[:, kk, 128 * t:128 * t + 128],
                              Woh[:, kk, :], Wol[:, kk, :], kk == 0, kk == 3, *h6, h_wos, *free)
                k = 4 * b + t
                d = DVE.do(lambda e: e.scalar_tensor_tensor(acc[:, k, :], ps[:, bank, :], tg[:, 0:1], acc[:, k, :], ALU.mult, ALU.add), h, h_xb[k])
                ra.read_by(i, d)
            a_free[:] = [h]

        h6 = []
        for G in range(NG):
            b, g, s = G // 4, G % 4, G % 2
            units = []
            if G + 1 < NG:
                units, negated, rows = max_units(G + 1)
            pslot, hexp, p_used = {}, {}, {}
            nu = 0
            h_sacc = None

            def unit(n):
                nonlocal nu
                for _ in range(n):
                    if nu < len(units):
                        units[nu]()
                        nu += 1

            def scores(kt, pr):
                m = 128 if kt < 12 else 65
                pt = P[pslot[kt]]
                bank, i, free = rb.take()
                for jj in range(2):
                    j = 2 * pr + jj
                    h = PE.do(lambda e: e.matmul(ps[:m, bank + jj, :], Kst[s][0:100, j, 128 * kt:128 * kt + m], Qst[s][0:100, j, :],
                                                 start=True, stop=True), h_k[G, pr], h_q[G], h_indk, mdone[G], *free, mark=(jj == 1))
                h = ACTQ.do(lambda e: e.activation(pt[:m, 2 * pr:2 * pr + 2, :], ps[:m, bank:bank + 2, :], ACT.Exp, scale=SCALE),
                            h, *p_free[pslot[kt]])
                rb.read_by(i, h)
                hexp[kt].append(h)

            def heads(bank, w, pt, p0, p1_, first, last, *waits):
                for j in range(4):
                    h = PE.do(lambda e: e.matmul(ps[32 * j:32 * j + 32, bank, :], w(j), pt[p0:p1_, j, :], start=first, stop=last,
                                                 tile_position=(p0, 32 * j)), *waits, *(o_free if first else []), mark=(j == 3))
                return h

            def weigh(kt, p0, p1_, first, last):
                h = heads(6, lambda j: Vg[s][p0:p1_, kt, 32 * j:32 * j + 32], P[pslot[kt]], p0, p1_, first, last, h_v[G], *hexp[kt])
                p_used[kt] = h
                p_free[pslot[kt]] = [h]
                return h

            def total(kt, p0, p1_, first, last):
                h = heads(7, lambda j: ones[p0:p1_, :], P[pslot[kt]], p0, p1_, first, last, h_ones, *hexp[kt])
                p_free[pslot[kt]] = [h]
                return h

            def add_on_pool(kt):
                nonlocal h_sacc
                i = ON_POOL.index(kt)
                if i == 0:
                    return
                x = P[pslot[ON_POOL[0]]] if i == 1 else sacc
                w = hexp[ON_POOL[0]] if i == 1 else [h_sacc]
                h_sacc = POOL.do(lambda e: e.tensor_tensor(sacc[:], x[:], P[pslot[kt]][:], ALU.add), *w, *hexp[kt], sacc_free)
                if i == 1:
                    p_free[pslot[ON_POOL[0]]].append(h_sacc)
                p_free[pslot[kt]].append(h_sacc)

            for kt in range(NKT):
                pslot[kt] = npt % 4
                npt += 1
                hexp[kt] = []
                nun = 0 if kt == 0 else 7 if kt < 10 else 1
                scores(kt, 0)
                unit(min(nun, 2))
                scores(kt, 1)
                unit(min(max(nun - 2, 0), 2))
                if kt == 3 and due:
                    project(*due.pop())
                if 1 <= kt <= 10:
                    p = kt - 1
                    weigh(p, 0, 128, p == 0, False)
                    unit(min(max(nun - 4, 0), 2))
                    if p in ON_POOL:
                        add_on_pool(p)
                    else:
                        total(p, 0, 128, p == 3, False)
                elif kt == 11:
                    weigh(10, 0, 64, False, True)
                    total(10, 0, 64, False, False)
                    h = heads(7, lambda j: ones[:, :], sacc, 0, 128, False, True, h_sacc)
                    sacc_free = h
                    h1 = ACTQ.do(lambda e: e.activation(ot[:], ps[:, 6, :], ACT.Copy), h, ot_free)
                    h2 = ACTQ.do(lambda e: e.activation(rt[:], ps[:, 7, :], ACT.Copy), h, ot_free)
                    o_free = [h1, h2]
                elif kt == 12:
                    weigh(10, 64, 128, True, False)
                    total(10, 64, 128, True, False)
                    weigh(11, 0, 128, False, False)
                    total(11, 0, 128, False, False)
                unit(max(nun - 6, 0))
                if kt == 10 and units:
                    unit(64)
                    negated()
                if kt == 11 and units:
                    rows()
            kst_last = (PE.sem, PE.n)
            weigh(12, 0, 65, False, True)
            h = total(12, 0, 65, False, True)
            kst_free[s] = qst_free[s] = vg_free[s] = [h]
            h1 = DVE.do(lambda e: e.tensor_tensor(oi[:], ps[:, 6, :], rt[:], ALU.mult), h, h2, *h6)
            h3 = DVE.do(lambda e: e.tensor_tensor(ot[:], ot[:], ps[:, 7, :], ALU.mult), h, h2)
            h4 = DVE.do(lambda e: e.tensor_tensor(pp[:], rt[:], ps[:, 7, :], ALU.mult), h, h2)
            o_free = [h1, h3, h4]
            ot_free = h4
            h5 = DVE.do(lambda e: e.reciprocal(rr[:], pp[:]), h4)
            hc = POOL.do(lambda e: e.tensor_tensor(oi[:], oi[:], ot[:], ALU.add), h1, h3)
            hd = POOL.do(lambda e: e.tensor_tensor(oi[:], oi[:], rr[:], ALU.mult), hc, h5)
            ot_free = hd
            he = ACTQ.do(lambda e: e.activation(aTh[:, g, :], oi[:], ACT.Copy), hd, *a_free)
            hf = POOL.do(lambda e: e.tensor_tensor(aTl[:, g, :], oi[:], aTh[:, g, :].bitcast(F32), ALU.subtract), he, *a_free)
            h6 = [he, hf]
            if G + 2 < NG:
                load_group(G + 2)
            if g == 3:
                due.append((b, h6))
        project(*due.pop())
        p2.close()
        barrier()

        p3 = ExitStack()
        xTh = sb(p3, "xTh", [128, 4, 2048], F32R)
        xTl = sb(p3, "xTl", [128, 4, 2048], F32R)
        gur = [sb(p3, f"gur{i}", [128, 4, 512], F32) for i in range(1)]
        dnr = [sb(p3, f"dnr{i}", [128, 2, 512], F32) for i in range(1)]
        guh = [sb(p3, f"guh{i}", [128, 4, 512], F32R) for i in range(2)]
        gul = [sb(p3, f"gul{i}", [128, 4, 512], F32R) for i in range(2)]
        dnh = [sb(p3, f"dnh{i}", [128, 2, 512], F32R) for i in range(2)]
        dnl = [sb(p3, f"dnl{i}", [128, 2, 512], F32R) for i in range(2)]
        ah = [sb(p3, f"ah{i}", [128, 2, 512], F32R) for i in range(2)]
        al = [sb(p3, f"al{i}", [128, 2, 512], F32R) for i in range(2)]
        sg = sb(p3, "sg", [128, 2, 512], F32)
        af = sb(p3, "af", [128, 2, 512], F32)
        xn3 = sb(p3, "xn3", [128, 2, D], F32)
        gtr = sb(p3, "gtr", [128, 4, NE], F32)
        gth = sb(p3, "gth", [128, 4, NE], F32R)
        gtl = sb(p3, "gtl", [128, 4, NE], F32R)
        iot = sb(p3, "iot", [128, NE], F32)
        cmb = sb(p3, "cmb", [128, 16, NE], F32)
        st3 = sb(p3, "st3", [128, 16, 12], F32)
        lg = sb(p3, "lg", [128, 16, NE], F32)
        lm = sb(p3, "lm", [128, 16, NE], F32)
        li = sb(p3, "li", [128, 16, NE], U32)
        wt = sb(p3, "wt", [128, 16, 8], F32)

        s_c3, s_gu, s_out = slot("s_c3"), slot("s_gu"), slot("s_out")
        SP.dma(s_c3, lambda e: e.dma_start(iot[:], ap["iota8"]))
        h_gt = SP.dma(s_c3, lambda e: e.dma_start(gtr[:], ap["w_gate"].rearrange("(k p) n -> p k n", p=128)))
        a = ACTQ.do(lambda e: e.activation(gth[:], gtr[:], ACT.Copy), h_gt)
        h_gts = DVE.do(lambda e: e.tensor_sub(gtl[:], gtr[:], gth[:].bitcast(F32)), a)

        NX = 12
        raw3_free = []
        wx_free = [[], []]
        h_wx = {}

        def load_expert(x):
            nonlocal raw3_free
            s = x % 2
            if x < NE:
                h = SP.dma(s_gu, lambda e: e.dma_start(gur[0][:], ap["w_gate_up"][x].rearrange("(k p) f -> p k f", p=128)), *raw3_free)
                h = SP.dma(s_gu, lambda e: e.dma_start(dnr[0][:], ap["w_down"][x].rearrange("(k p) h -> p k h", p=128)))
            else:
                y = x - NE
                w = ap["w_sh_gate_up"].rearrange("(k p) f -> p k f", p=128)
                SP.dma(s_gu, lambda e: e.dma_start(gur[0][:, :, 0:256], w[:, :, 256 * y:256 * y + 256]), *raw3_free)
                SP.dma(s_gu, lambda e: e.dma_start(gur[0][:, :, 256:512], w[:, :, 1024 + 256 * y:1280 + 256 * y]))
                h = SP.dma(s_gu, lambda e: e.dma_start(dnr[0][:], ap["w_sh_down"][256 * y:256 * y + 256, :].rearrange("(k p) h -> p k h", p=128)))
            a = ACTQ.do(lambda e: e.activation(guh[s][:], gur[0][:], ACT.Copy), h, *wx_free[s])
            b_ = ACTQ.do(lambda e: e.activation(dnh[s][:], dnr[0][:], ACT.Copy), h)
            c = POOL.do(lambda e: e.tensor_tensor(gul[s][:], gur[0][:], guh[s][:].bitcast(F32), ALU.subtract), a, *wx_free[s])
            d = POOL.do(lambda e: e.tensor_tensor(dnl[s][:], dnr[0][:], dnh[s][:].bitcast(F32), ALU.subtract), b_)
            raw3_free = [a, b_, c, d]
            h_wx[x] = [a, b_, c, d]

        load_expert(0)
        tr3 = Banks([0, 1])
        h_xt, xn3_free, h_cmb = [], [None] * 2, []
        for k in range(16):
            xs = k % 2
            a = DVE.do(lambda e, k=k: e.bn_stats(st3[:, k, 0:6], acc[:, k, :]))
            a = DVE.do(lambda e, k=k: e.bn_aggr(st3[:, k, 6:8], st3[:, k, 0:6]), a)
            a = DVE.do(lambda e, k=k: e.tensor_scalar(st3[:, k, 8:9], st3[:, k, 7:8], 1e-5, None, ALU.add), a)
            c = ACTQ.do(lambda e, k=k: e.activation(st3[:, k, 9:10], st3[:, k, 8:9], ACT.Sqrt), a)
            d = DVE.do(lambda e, k=k: e.reciprocal(st3[:, k, 10:11], st3[:, k, 9:10]), c)
            d = DVE.do(lambda e, k=k, xs=xs: e.tensor_scalar(xn3[:, xs, :], acc[:, k, :], st3[:, k, 6:7], st3[:, k, 10:11], ALU.subtract, ALU.mult), d, xn3_free[xs])
            bank, i, free = tr3.take()
            for g in range(4):
                h = PE.do(lambda e, g=g, xs=xs, bank=bank: e.transpose(ps[:, bank, 128 * g:128 * g + 128], xn3[:, xs, 128 * g:128 * g + 128], ident[:]), d, *free, mark=(g == 3))
            xn3_free[xs] = h
            v = ps[:, bank, :].rearrange("p (g s) -> p g s", g=4)
            hi, lo = xTh[:, :, 128 * k:128 * k + 128], xTl[:, :, 128 * k:128 * k + 128]
            a = ACTQ.do(lambda e, hi=hi, v=v: e.activation(hi, v, ACT.Copy), h)
            d = DVE.do(lambda e, hi=hi, lo=lo, v=v: e.tensor_sub(lo, v, hi.bitcast(F32)), a)
            tr3.read_by(i, a)
            tr3.read_by(i, d)
            h_xt.append((a, d))
        lg3 = Banks([2, 3])
        for k in range(16):
            bank, i, free = lg3.take()
            for kk in range(4):
                h = three(ps[:, bank, 0:NE], xTh[:, kk, 128 * k:128 * k + 128], xTl[:, kk, 128 * k:128 * k + 128],
                          gth[:, kk, :], gtl[:, kk, :], kk == 0, kk == 3, *h_xt[k], h_gts, *free)
            d = DVE.do(lambda e, k=k, bank=bank: e.tensor_copy(lg[:, k, :], ps[:, bank, 0:NE]), h)
            lg3.read_by(i, d)
            d = DVE.do(lambda e, k=k: e.max(lm[:, k, :], lg[:, k, :]), d)
            d = DVE.do(lambda e, k=k: e.max_index(li[:, k, :], lm[:, k, :], lg[:, k, :]), d)
        h_li = d
        a = DVE.do(lambda e: e.tensor_sub(wt[:, :, 0], lm[:, :, 1], lm[:, :, 0]), h_li)
        c = ACTQ.do(lambda e: e.activation(wt[:, :, 1], wt[:, :, 0], ACT.Exp), a)
        a = DVE.do(lambda e: e.tensor_scalar(wt[:, :, 2], wt[:, :, 1], 1.0, None, ALU.add), c)
        a = DVE.do(lambda e: e.reciprocal(wt[:, :, 3], wt[:, :, 2]), a)
        a = DVE.do(lambda e: e.tensor_scalar(wt[:, :, 4], wt[:, :, 3], tg[:, 1:2], None, ALU.mult), a)
        a = DVE.do(lambda e: e.tensor_tensor(wt[:, :, 5], wt[:, :, 4], wt[:, :, 1], ALU.mult), a)
        a = DVE.do(lambda e: e.tensor_copy(wt[:, :, 6:8], li[:, :, 0:2]), a, h_li)
        for k in range(16):
            d = DVE.do(lambda e, k=k: e.tensor_scalar(lg[:, k, :], iot[:], wt[:, k, 7:8], wt[:, k, 5:6], ALU.is_equal, ALU.mult), a, h_gt)
            d = DVE.do(lambda e, k=k: e.tensor_scalar(cmb[:, k, :], iot[:], wt[:, k, 6:7], wt[:, k, 4:5], ALU.is_equal, ALU.mult), d)
            d = DVE.do(lambda e, k=k: e.tensor_tensor(cmb[:, k, :], cmb[:, k, :], lg[:, k, :], ALU.add), d)
        h_cmb = d

        up3, dn3 = Banks([0, 1, 2, 3, 4]), Banks([5, 6, 7])
        first_waits = [h for pair in h_xt for h in pair] + [h_cmb]
        a_free3 = [[], []]
        sg_free, af_free = [None] * 2, [[] for _ in range(2)]
        pend = None
        acc_last = [None] * 16
        nstep = 0

        def down(x, tb, s, hact):
            w = x % 2
            for t in range(4):
                bank, i, free = dn3.take()
                k = 4 * tb + t
                for kk in range(2):
                    h = three(ps[:, bank, :], ah[s][:, kk, 128 * t:128 * t + 128], al[s][:, kk, 128 * t:128 * t + 128],
                              dnh[w][:, kk, :], dnl[w][:, kk, :], kk == 0, kk == 1, *hact, *h_wx[x], *free)
                sc = cmb[:, k, x:x + 1] if x < NE else tg[:, 1:2]
                d = DVE.do(lambda e, k=k, bank=bank, sc=sc: e.scalar_tensor_tensor(acc[:, k, :], ps[:, bank, :], sc, acc[:, k, :], ALU.mult, ALU.add), h, acc_last[k])
                dn3.read_by(i, d)
                acc_last[k] = d
            a_free3[s] = [h]
            if tb == 3:
                wx_free[w] = [h]
                if x + 2 < NX:
                    load_expert(x + 2)
            if x == NX - 1:
                for t in range(4):
                    k = 4 * tb + t
                    SP.dma(s_out, lambda e, k=k: e.dma_start(ap["out"].rearrange("b (t p) d -> p (b t) d", p=128)[:, k, :], acc[:, k, :]), acc_last[k])

        load_expert(1)
        for x in range(NX):
            w = x % 2
            for tb in range(4):
                s = nstep % 2
                nstep += 1
                hact = []
                for f in range(2):
                    got = []
                    for half in range(2):
                        bank, i, free = up3.take()
                        c0 = 256 * half + 128 * f
                        for kk in range(4):
                            h = three(ps[:, bank, :], guh[w][:, kk, c0:c0 + 128], gul[w][:, kk, c0:c0 + 128],
                                      xTh[:, kk, 512 * tb:512 * tb + 512], xTl[:, kk, 512 * tb:512 * tb + 512], kk == 0, kk == 3,
                                      *h_wx[x], *first_waits, *free)
                        got.append((bank, i, h))
                    (bg, ig, hg), (bu, iu, hu) = got
                    a = ACTQ.do(lambda e, f=f, bg=bg: e.activation(sg[:, f, :], ps[:, bg, :], ACT.Silu), hg, sg_free[f])
                    up3.read_by(ig, a)
                    d = DVE.do(lambda e, f=f, bu=bu: e.tensor_tensor(af[:, f, :], sg[:, f, :], ps[:, bu, :], ALU.mult), a, hu, *af_free[f])
                    up3.read_by(iu, d)
                    sg_free[f] = d
                    c = ACTQ.do(lambda e, f=f, s=s: e.activation(ah[s][:, f, :], af[:, f, :], ACT.Copy), d, *a_free3[s])
                    g_ = DVE.do(lambda e, f=f, s=s: e.tensor_sub(al[s][:, f, :], af[:, f, :], ah[s][:, f, :].bitcast(F32)), c, *a_free3[s])
                    af_free[f] = [g_]
                    hact += [c, g_]
                if pend:
                    down(*pend)
                pend = (x, tb, s, hact)
        down(*pend)
        SP.wait((s_out.sem, s_out.n))
        for s in slots:
            SP.wait((s.sem, s.n))

        p3.close()


def kernel(**inputs):
    import concourse.bacc as _bacc
    from concourse.bass_utils import run_bass_kernel_spmd as _run

    def X(n):
        return np.asarray(inputs[n])

    c = X("ctx_2048")
    ctxT = np.ascontiguousarray(np.concatenate([c[:, NIMG:], c[:, :NIMG]], axis=1).transpose(0, 2, 1))
    ind = np.zeros((4, NKP), np.float32)
    ind[0:2, :NTXT] = 1.0
    ind[2:4, NTXT:] = 1.0
    arrays = {
        "x": X("x"), "ctxT": ctxT, "g_xattn": X("g_xattn"), "g_ffn": X("g_ffn"),
        "ident": np.eye(128, dtype=np.float32), "ind": ind,
        "iota8": np.ascontiguousarray(np.broadcast_to(np.arange(8, dtype=np.float32), (128, 8))),
        "w_gate": X("L0_ffn_w_gate"), "w_gate_up": X("L0_ffn_w_gate_up"), "w_down": X("L0_ffn_w_down"),
        "w_sh_gate_up": X("L0_ffn_w_sh_gate_up"), "w_sh_down": X("L0_ffn_w_sh_down"),
    }
    for n in ("q_b", "k_b", "v_b", "k_img_b", "v_img_b", "o_b", "norm_q_w", "norm_k_w", "norm_k_img_w"):
        arrays[n] = X("L0_xattn_" + n)
    for n in ("q_w", "k_w", "v_w", "k_img_w", "v_img_w", "o_w"):
        arrays[n + "T"] = np.ascontiguousarray(X("L0_xattn_" + n).T)

    nc = _bacc.Bacc("TRN2", target_bir_lowering=False, num_devices=1)
    ins, ap = {}, {}
    for name, a in arrays.items():
        a = np.ascontiguousarray(a)
        ins["in_" + name] = a
        ap[name] = nc.dram_tensor("in_" + name, a.shape, mybir.dt.from_np(a.dtype), kind="ExternalInput").ap()
    ap["out"] = nc.dram_tensor("out_0", (NB, LQ, D), F32, kind="ExternalOutput").ap()
    flamingo_program(nc, ap)
    r = _run(nc, [ins], core_ids=[0])
    return r.results[0]["out_0"]
```

```python
import numpy as np
from contextlib import ExitStack

import concourse.bass as bass
from concourse import mybir

F32 = mybir.dt.float32
F32R = mybir.dt.float32r
U32 = mybir.dt.uint32
ACT = mybir.ActivationFunctionType
ALU = mybir.AluOpType
AX = mybir.AxisListType

NB = 4
D = 512
LQ = 512
NTXT, NIMG = 1344, 257
NK = NTXT + NIMG
NKP = NK + 1
NKT = 13
SCALE = 1.0 / float(np.sqrt(np.float32(32.0)))
NE = 8


class Queue:

    def __init__(self, eng, sem):
        self.eng, self.sem, self.n, self.seen = eng, sem, 0, {}

    def wait(self, *handles):
        for h in handles:
            if h is not None and self.seen.get(h[0].name, 0) < h[1]:
                self.eng.wait_ge(*h)
                self.seen[h[0].name] = h[1]

    def do(self, fn, *waits, mark=True):
        self.wait(*waits)
        ins = fn(self.eng)
        if mark:
            ins.then_inc(self.sem, 1)
            self.n += 1
            return (self.sem, self.n)
        return None

    def dma(self, slot, fn, *waits):
        self.wait(*waits)
        fn(self.eng).then_inc(slot.sem, 16)
        slot.n += 16
        return (slot.sem, slot.n)


class Slot:

    def __init__(self, sem):
        self.sem, self.n = sem, 0


class Banks:

    def __init__(self, banks):
        self.banks, self.at, self.readers = banks, 0, [[] for _ in banks]

    def take(self):
        i = self.at % len(self.banks)
        self.at += 1
        r, self.readers[i] = self.readers[i], []
        return self.banks[i], i, r

    def read_by(self, i, handle):
        self.readers[i].append(handle)


def flamingo_program(nc, ap):
    ctx = ExitStack()
    with ctx:
        def sem(name):
            return ctx.enter_context(nc.semaphore(name))

        PE, DVE, ACTQ, POOL, SP = (Queue(e, sem(n)) for e, n in (
            (nc.tensor, "c_pe"), (nc.vector, "c_dve"), (nc.scalar, "c_act"), (nc.gpsimd, "c_pool"), (nc.sync, "c_sp")))
        slots = []

        def slot(name):
            slots.append(Slot(sem(name)))
            return slots[-1]

        def sb(stack, name, shape, dt):
            return stack.enter_context(nc.sbuf_tensor(name, shape, dt))

        ps = ctx.enter_context(nc.psum_tensor("ps", [128, 8, 512], F32))

        KHd = nc.dram_tensor("KHd", (NB, D, NKP), F32).ap()
        KLd = nc.dram_tensor("KLd", (NB, D, NKP), F32).ap()
        Vd = nc.dram_tensor("Vd", (NB, NK, D), F32).ap()
        QHd = nc.dram_tensor("QHd", (NB, D, LQ), F32).ap()
        QLd = nc.dram_tensor("QLd", (NB, D, LQ), F32).ap()

        def barrier(*but):
            h = [(q.sem, q.n) for q in (PE, DVE, ACTQ, POOL) if q.n] + [(s.sem, s.n) for s in slots if s.n and s not in but]
            for q in (PE, DVE, ACTQ, POOL, SP):
                q.wait(*h)

        def three(out, ah, al, bh, bl, first, last, *waits):
            PE.do(lambda e: e.matmul(out, ah, bh, start=first, stop=False), *waits, mark=False)
            PE.do(lambda e: e.matmul(out, ah, bl, start=False, stop=False), mark=False)
            return PE.do(lambda e: e.matmul(out, al, bh, start=False, stop=last), mark=last)

        ident = sb(ctx, "ident", [128, 128], F32)
        acc = sb(ctx, "acc", [128, 16, D], F32)
        tg = sb(ctx, "tg", [128, 2], F32)
        gin = sb(ctx, "gin", [128, 2], F32)
        st3 = sb(ctx, "st3", [128, 16, 12], F32)
        h_st3 = {}
        s_c = slot("s_c")
        h_id = SP.dma(s_c, lambda e: e.dma_start(ident[:], ap["ident"]))
        SP.dma(s_c, lambda e: e.dma_start(gin[:, 0:1], ap["g_xattn"].partition_broadcast(128)))
        h_g = SP.dma(s_c, lambda e: e.dma_start(gin[:, 1:2], ap["g_ffn"].partition_broadcast(128)))
        h_id = h_g
        h_tg = ACTQ.do(lambda e: e.activation(tg[:], gin[:], ACT.Tanh), h_g)

        Kst = [sb(ctx, "Kst0", [128, 4, NKP], F32R)]
        Qst = [sb(ctx, "Qst0", [128, 4, LQ], F32R)]
        kflat = Kst[0][:].rearrange("p a b -> p (a b)")

        def in_kst0(at, k, n):
            return kflat[:, at:at + k * n].rearrange("p (k n) -> p k n", k=k)

        mp = sb(ctx, "mp", [128, 16, 4], F32)
        mx = sb(ctx, "mx", [128, 16, 2], F32)
        mn = sb(ctx, "mn", [128, 4, 4, 4], F32R)
        mrow = sb(ctx, "mrow", [16, LQ], F32R)

        p1 = ExitStack()
        bias = sb(p1, "bias", [128, 8, D], F32)
        QB, QNW, KB, KNW, VB, KIB, KINW, VIB = range(8)
        Whs = sb(p1, "Whs", [128, 4, 4, D], F32R)
        Wls = sb(p1, "Wls", [128, 4, 4, D], F32R)
        WQ, WK, WV, WKI, WVI = range(5)
        Wh = [in_kst0(0, 4, D)] + [Whs[:, i] for i in range(4)]
        Wl = [in_kst0(2048, 4, D)] + [Wls[:, i] for i in range(4)]
        raw = sb(p1, "raw", [128, 2, 4, 256], F32)
        wraw = raw[:].rearrange("p a b c -> p (a b c)").rearrange("p (k o) -> p k o", k=4)
        ch = sb(p1, "ch", [128, 2, 4, 256], F32R)
        cl = sb(p1, "cl", [128, 2, 4, 256], F32R)
        kf = sb(p1, "kf", [128, 4, D], F32)
        lnst = sb(p1, "lnst", [128, 16, 4], F32)
        vf = sb(p1, "vf", [128, 2, D], F32)
        junk = sb(p1, "junk", [128, D], F32)
        sth = sb(p1, "sth", [128, 2, 4, 258], F32R)
        stl = sb(p1, "stl", [128, 2, 4, 258], F32R)
        xn = sb(p1, "xn", [128, 2, D], F32)
        st = sb(p1, "st", [128, 8, 8], F32)
        bst = sb(p1, "bst", [128, 8, 6], F32)

        s_ob, s_ind = slot("s_ob"), slot("s_ind")
        s_b, s_x0, s_x1, s_x2, s_w = slot("s_b"), slot("s_x0"), slot("s_x1"), slot("s_x2"), slot("s_w")
        s_raw = [slot(f"s_raw{i}") for i in range(2)]
        s_st = [slot(f"s_st{i}") for i in range(2)]
        s_v = [slot(f"s_v{i}") for i in range(2)]

        xv = ap["x"].rearrange("b (t p) d -> p (b t) d", p=128)
        h_x = [SP.dma(s_x0, lambda e: e.dma_start(acc[:, 0:4, :], xv[:, 0:4, :]))]
        wsplit, wfree = {}, None

        def fetch_w(name):
            return SP.dma(s_w, lambda e: e.dma_start(wraw, ap[name].rearrange("(k p) o -> p k o", p=128)), wfree)

        def split_w(w, h, lo, k0=0, k1=4):
            nonlocal wfree
            k = slice(k0, k1)
            hh = ACTQ.do(lambda e: e.activation(Wh[w][:, k], wraw[:, k], ACT.Copy), h)
            wfree = lo.do(lambda e: e.tensor_tensor(Wl[w][:, k], wraw[:, k], Wh[w][:, k].bitcast(F32), ALU.subtract), h, hh)
            wsplit[w] = (hh, wfree)

        h_wq = fetch_w("q_wT")
        h_x.append(SP.dma(s_x1, lambda e: e.dma_start(acc[:, 4:8, :], xv[:, 4:8, :])))
        names = ["q_b", "norm_q_w", "k_b", "norm_k_w", "v_b", "k_img_b", "norm_k_img_w", "v_img_b"]
        for i, n in enumerate(names):
            h_bias = SP.dma(s_b, lambda e: e.dma_start(bias[:, i, :], ap[n].partition_broadcast(128)))
        h_x += [SP.dma(s_x2, lambda e: e.dma_start(acc[:, 8:16, :], xv[:, 8:16, :]))] * 2
        later_w = [(WK, "k_wT"), (WV, "v_wT"), (WKI, "k_img_wT"), (WVI, "v_img_wT")]

        ra = Banks([0, 1])
        mm, tr = Banks(range(2, 6)), Banks([6, 7, 0, 1])
        nst = 0
        st_last = [None] * 8

        def square(src, rows, row_wait):
            nonlocal nst
            r = nst % 8
            nst += 1
            a = ACTQ.do(lambda e: e.activation(junk[:rows], src, ACT.Square, accum_out=st[:rows, r, 0:1]),
                        row_wait, st_last[r], (ACTQ.sem, ACTQ.n))
            return r, a

        def root(rows, sq):
            r, a = sq
            b_ = DVE.do(lambda e: e.tensor_scalar(st[:rows, r, 1:2], st[:rows, r, 0:1], 1.0 / D, 1e-6, ALU.mult, ALU.add), a)
            return r, ACTQ.do(lambda e: e.activation(st[:rows, r, 2:3], st[:rows, r, 1:2], ACT.Sqrt), b_)

        def rms_scale(src, rows, root, parts):
            r, c = root
            d = DVE.do(lambda e: e.reciprocal(st[:rows, r, 3:4], st[:rows, r, 2:3]), c)
            for p0, p1_, nw in parts:
                h = DVE.do(lambda e: e.scalar_tensor_tensor(src[p0:p1_], src[p0:p1_], st[p0:p1_, r, 3:4], bias[p0:p1_, nw, :], ALU.mult, ALU.mult), d)
            st_last[r] = h
            return h

        kf_free, vf_free = [None] * 4, [None] * 2
        st_free = [[] for _ in range(2)]
        nkf = nvf = 0

        def transposed(src, rows, src_wait, hi, lo, dst_waits):
            bank, i, free = tr.take()
            for g in range(4):
                h = PE.do(lambda e, g=g: e.transpose(ps[:, bank, g * 128:g * 128 + rows], src[:, g * 128:g * 128 + 128], ident[:rows, :rows]),
                          src_wait, h_id, *free, mark=(g == 3))
            v = ps[:, bank, :].rearrange("p (g s) -> p g s", g=4)[:, :, 0:rows]
            a = ACTQ.do(lambda e: e.activation(hi, v, ACT.Copy), h, *dst_waits)
            d = DVE.do(lambda e: e.tensor_sub(lo, v, hi.bitcast(F32)), a, *dst_waits)
            tr.read_by(i, a)
            tr.read_by(i, d)
            return a, d, h

        xn_free = [None] * 2
        ch_free = [None] * 2
        q_done = []

        def finish_q(b, t, slot3, hnorm):
            s, c0 = (t // 2) % 2, 128 * (t % 2)
            a, d, ht = transposed(kf[:, slot3, :], 128, hnorm, sth[:, s, :, c0:c0 + 128], stl[:, s, :, c0:c0 + 128], st_free[s])
            kf_free[slot3] = ht
            q_done.extend([a, d])
            if t % 2:
                for src, dst in ((sth, QHd), (stl, QLd)):
                    st_free[s] = [SP.dma(s_st[s], lambda e, src=src, dst=dst: e.dma_start(
                        dst[b].rearrange("(k p) s -> p k s", p=128)[:, :, 256 * s:256 * s + 256], src[:, s, :, 0:256].bitcast(F32)), *q_done)]
                q_done.clear()

        h_ln = {}

        def ln_stats(k):
            h_bn[k] = DVE.do(lambda e: e.bn_stats(bst[:, k % 8, :], acc[:, k, :]), h_x[k // 4])

        def ln_finish(b):
            for k in range(4 * b, 4 * b + 4):
                a = DVE.do(lambda e: e.bn_aggr(lnst[:, k, 0:2], bst[:, k % 8, :]), h_bn[k])
            v = lnst[:, 4 * b:4 * b + 4, :]
            a = DVE.do(lambda e: e.tensor_scalar(v[:, :, 2], v[:, :, 1], 1e-5, None, ALU.add), a)
            c = ACTQ.do(lambda e: e.activation(v[:, :, 3], v[:, :, 2], ACT.Sqrt), a)
            h_ln[b] = DVE.do(lambda e: e.reciprocal(v[:, :, 2], v[:, :, 3]), c)

        h_bn = {}
        for k in range(4):
            ln_stats(k)
        ln_finish(0)
        ctf = ap["ctxT"]
        raw_free = [[], []]
        chunks = [(b, c) for b in range(NB) for c in range(7)]
        h_raw, h_split = {}, {}

        def load_chunk(n):
            (b, c), s = chunks[n], n % 2
            w = 256 if c < 6 else 65
            h_raw[n] = SP.dma(s_raw[s], lambda e: e.dma_start(
                raw[:, s, :, 0:w], ctf[b].rearrange("(k p) s -> p k s", p=128)[:, :, 256 * c:256 * c + w]), *raw_free[s])

        def split_chunk(n):
            (b, c), s = chunks[n], n % 2
            w = 256 if c < 6 else 65
            hh = ACTQ.do(lambda e: e.activation(ch[:, s, :, 0:w], raw[:, s, :, 0:w], ACT.Copy), h_raw[n], ch_free[s])
            hl = POOL.do(lambda e: e.tensor_tensor(cl[:, s, :, 0:w], raw[:, s, :, 0:w], ch[:, s, :, 0:w].bitcast(F32), ALU.subtract), h_raw[n], hh, ch_free[s])
            raw_free[s] = [hh, hl]
            h_split[n] = (hh, hl)

        h_xn, h_xT, roots, scaled = {}, {}, {}, {}

        def centred(k):
            h_xn[k] = DVE.do(lambda e: e.tensor_scalar(xn[:, k % 2, :], acc[:, k, :], lnst[:, k, 0:1], lnst[:, k, 2:3], ALU.subtract, ALU.mult),
                              h_ln[k // 4], xn_free[k % 2])

        centred(0)
        centred(1)
        KF = {}
        for i in range(-1, 17):
            k = i + 1
            if 0 <= k < 16:
                xs = k % 2
                a, d, ht = transposed(xn[:, xs, :], 128, h_xn[k], ch[:, xs, :, 0:128], cl[:, xs, :, 0:128], [ch_free[xs]])
                xn_free[xs] = ht
                h_xT[k] = (a, d)
                if k == 0:
                    split_w(WQ, h_wq, DVE)
            k = i + 3
            if 2 <= k < 16:
                if k % 4 == 0:
                    ln_finish(k // 4)
                centred(k)
            k = i
            if 0 <= k < 16:
                xs = k % 2
                bank, bi, free = mm.take()
                for kk in range(4):
                    hq = three(ps[:, bank, :], ch[:, xs, kk, 0:128], cl[:, xs, kk, 0:128], Wh[WQ][:, kk, :], Wl[WQ][:, kk, :],
                               kk == 0, kk == 3, *h_xT[k], *wsplit[WQ], *free)
                ch_free[xs] = hq
                s3 = KF[k] = nkf % 4
                nkf += 1
                h = DVE.do(lambda e: e.tensor_tensor(kf[:, s3, :], ps[:, bank, :], bias[:, QB, :], ALU.add), hq, h_bias, kf_free[s3])
                mm.read_by(bi, h)
                sq = square(kf[:, s3, :], 128, h)
            for k in {-1: (4, 5), 0: (6, 7)}.get(i, (i + 7,) if 1 <= i < 9 else ()):
                ln_stats(k)
            k = i - 1
            if 0 <= k < 16:
                scaled[k] = rms_scale(kf[:, KF[k], :], 128, roots[k], [(0, 128, QNW)])
            if 0 <= i < 16:
                roots[i] = root(128, sq)
            k = i - 2
            if 0 <= k < 14:
                finish_q(k // 4, k % 4, KF[k], scaled[k])
            if i == 14:
                split_chunk(0)
            if i > 0 and i % 3 == 2 and w_on_way:
                split_w(*w_on_way, POOL, 0, 2)
            if i >= 0 and i % 3 == 0:
                if i and w_on_way:
                    split_w(*w_on_way, POOL, 2, 4)
                    w_on_way = None
                if later_w:
                    w_on_way = (later_w[0][0], fetch_w(later_w.pop(0)[1]))
            if i == 12:
                raw_free = [[wfree], [wfree]]
                load_chunk(0)
                load_chunk(1)

        ra.readers = tr.readers[2:]
        tr.banks, tr.readers = tr.banks[:2], tr.readers[:2]
        q_left = [lambda k=k: finish_q(k // 4, k % 4, KF[k], scaled[k]) for k in (14, 15)]

        s_k2 = [[slot(f"s_k2{i}{j}") for j in range(2)] for i in range(2)]
        s_q2 = [slot(f"s_q2{i}") for i in range(3)]
        s_v2 = [slot(f"s_v2{i}") for i in range(2)]
        s_m2 = [slot(f"s_m2{i}") for i in range(2)]
        s_c2, s_wo = slot("s_c2"), slot("s_wo")

        NG = 4 * NB
        kst_free = [[[], []] for _ in range(2)]
        qst_free = [[] for _ in range(3)]
        vg_free = [[] for _ in range(2)]
        h_k, h_q, h_v = {}, {}, {}

        KPART = [(0, 1280), (1280, NKP)]

        def head_rows(d, G):
            return d[G // 4, 128 * (G % 4):128 * (G % 4) + 128, :].rearrange("(j p) s -> p j s", p=32)

        def load_keys(G, part, *waits):
            s, (c0, c1) = G % 2, KPART[part]
            for p0, d in ((0, KHd), (32, KHd), (64, KLd)):
                h_k[G, part] = SP.dma(s_k2[s][part], lambda e: e.dma_start(
                    Kst[s][p0:p0 + 32, :, c0:c1].bitcast(F32), head_rows(d, G)[:, :, c0:c1]), *kst_free[s][part], *waits)

        def load_queries(G, *waits):
            for p0, d in ((0, QHd), (32, QLd), (64, QHd)):
                h_q[G] = SP.dma(s_q2[G % 3], lambda e: e.dma_start(Qst[G % 3][p0:p0 + 32].bitcast(F32), head_rows(d, G)), *qst_free[G % 3], *waits)

        def load_values(G):
            b, g, s = G // 4, G % 4, G % 2
            rows = slice(128 * g, 128 * g + 128)
            SP.dma(s_v2[s], lambda e: e.dma_start(
                Vg[s][:, 0:12, :], Vd[b, 0:1536, rows].rearrange("(t p) d -> p t d", p=128)), *vg_free[s])
            h_v[G] = SP.dma(s_v2[s], lambda e: e.dma_start(Vg[s][0:65, 12, :], Vd[b, 1536:NK, rows]))

        CH = [(0, 512), (512, 1024), (1024, NTXT), (NTXT, NKP)]
        mdone = {}

        def max_units(G):
            s = G % 2
            last = {}
            units = []
            blocks = [(j, qt) for j in range(4) for qt in range(4)]
            long = [(c, *x) for c in (0, 1) for x in blocks]
            short = [(c, *x) for c in (2, 3) for x in blocks]
            order = long[:8]
            for i in range(32):
                order.append(short[i])
                if i % 4 != 3:
                    order.append(long[8 + i - i // 4])
            for c, j, qt in order:
                def unit(c=c, j=j, qt=qt):
                    c0, c1 = CH[c]
                    bank, i, free = ra.take()
                    h = PE.do(lambda e: e.matmul(ps[:, bank, 0:c1 - c0], Qst[G % 3][0:96, j, 128 * qt:128 * qt + 128],
                                                 Kst[s][0:96, j, c0:c1], start=True, stop=True), h_k[G, int(c > 1)], h_q[G], *free)
                    h = DVE.do(lambda e: e.reduce_max(mp[:, 4 * qt + j, c:c + 1], ps[:, bank, 0:c1 - c0], AX.X), h)
                    ra.read_by(i, h)
                    last["h"] = h
                units.append(unit)

            hs = []

            def negated():
                a = DVE.do(lambda e: e.tensor_reduce(mx[:, :, 0], mp[:, :, 0:3], axis=AX.X, op=ALU.max), last["h"], mdone.get(("mn", G - 1)))
                b_ = DVE.do(lambda e: e.tensor_copy(mx[:, :, 1], mp[:, :, 3]), last["h"])
                for k in range(2):
                    m = mx[:, :, k].rearrange("p (q j) -> p q j", q=4)
                    c = DVE.do(lambda e: e.tensor_scalar(mn[:, :, 2 * k, :], m, -1.0, None, ALU.mult), a, b_)
                    hs.append(DVE.do(lambda e: e.scalar_tensor_tensor(mn[:, :, 2 * k + 1, :], m, -1.0, mn[:, :, 2 * k, :].bitcast(F32), ALU.mult, ALU.subtract), c))

            def rows_of_m():
                bank, i, free = ra.take()
                for qt in range(4):
                    h = PE.do(lambda e, qt=qt: e.transpose(ps[0:16, bank, 128 * qt:128 * qt + 128],
                                                           mn[:, qt].rearrange("p k j -> p (k j)").bitcast(F32), ident[:]), *hs, *free, mark=(qt == 3))
                mdone[("mn", G)] = h
                h = DVE.do(lambda e: e.tensor_copy(mrow[:], ps[0:16, bank, :]), h, mdone.get(("row", G - 1)))
                ra.read_by(i, h)
                mdone[G] = SP.dma(s_m2[s], lambda e: e.dma_start(Qst[G % 3][96:100].bitcast(F32), mrow[:].bitcast(F32)), h, *qst_free[G % 3])
                mdone[("row", G)] = mdone[G]
            return units, negated, rows_of_m

        k_pending = []
        nchunk = 0

        def finish_k(b, c, j, rows, s, s3, hnorm, last, width):
            c0 = 128 * j
            a, d, ht = transposed(kf[:rows, s3, :], rows, hnorm, sth[:, s, :, c0:c0 + rows], stl[:, s, :, c0:c0 + rows], st_free[s])
            kf_free[s3] = ht
            k_done.extend([a, d])
            if c == 6:
                k_done.append(ACTQ.do(lambda e: e.activation(sth[:, s, :, rows:rows + 1], sth[:, s, :, rows - 1:rows].bitcast(F32), ACT.Copy), a))
                k_done.append(DVE.do(lambda e: e.tensor_copy(stl[:, s, :, rows:rows + 1], stl[:, s, :, rows - 1:rows].bitcast(F32)), d))
            if last:
                for src, dst in ((sth, KHd), (stl, KLd)):
                    st_free[s] = [SP.dma(s_st[s], lambda e, src=src, dst=dst: e.dma_start(
                        dst[b].rearrange("(k p) s -> p k s", p=128)[:, :, 256 * c:256 * c + width],
                        src[:, s, :, 0:width].bitcast(F32)), *k_done)]
                k_done.clear()

        k_done = []
        h_indk, hx, hq_last = [], scaled[15], hq
        xflat = xn[96:100].rearrange("p a b -> p (a b)")

        def indicate(c0, c1):
            nonlocal hx
            h = SP.dma(s_ind, lambda e: e.dma_start(xflat[:, 0:c1 - c0], ap["ind"][:, c0:c1]), hx, *xn_free)
            for j in range(4):
                hx = ACTQ.do(lambda e: e.activation(Kst[0][96:100, j, c0:c1], xflat[:, 0:c1 - c0], ACT.Copy), h, *wsplit[WQ], hq_last)

        units0, rows0_due = [], False
        h_xb = []
        obb = bias[:, QB, :]
        h_ob = SP.dma(s_ob, lambda e: e.dma_start(obb, ap["o_b"].partition_broadcast(128)), scaled[15])
        for b in range(NB):
            for c in range(7):
                n = 256 if c < 6 else 65
                s = nchunk % 2
                if b == 0 and 1 <= c <= 4:
                    indicate(400 * c - 400, 400 * c if c < 4 else NKP)
                    if c == 4:
                        h_indk.append(hx)
                if (b, c) == (1, 3):
                    units0, negated0, rows0 = max_units(0)
                hh, hl = h_split[nchunk]
                if nchunk + 1 < len(chunks):
                    split_chunk(nchunk + 1)
                if nchunk + 2 < len(chunks):
                    load_chunk(nchunk + 2)
                if (b, c) == (1, 1):
                    stored = [(q.sem, q.n) for q in s_st]
                    load_keys(0, 0, *stored)
                    load_queries(0, *stored)
                    load_keys(0, 1, *stored)
                nchunk += 1
                for j in range(2 if c < 6 else 1):
                    rows = 128 if c < 6 else 65
                    t = 2 * c + j
                    if t < 10:
                        parts = [(0, 128, WK, WV, KB, KNW, VB)]
                    elif t == 10:
                        parts = [(0, 64, WK, WV, KB, KNW, VB), (64, 128, WKI, WVI, KIB, KINW, VIB)]
                    else:
                        parts = [(0, rows, WKI, WVI, KIB, KINW, VIB)]
                    s3 = nkf % 4
                    nkf += 1
                    hk = []
                    for p0, p1_, wk, wv, kb, knw, vb in parts:
                        bank, i, free = mm.take()
                        for kk in range(4):
                            hm = three(ps[:rows, bank, :], ch[:, s, kk, 128 * j:128 * j + rows], cl[:, s, kk, 128 * j:128 * j + rows],
                                       Wh[wk][:, kk, :], Wl[wk][:, kk, :], kk == 0, kk == 3, hh, hl, *wsplit[wk], *free)
                        h = DVE.do(lambda e, s3=s3, bank=bank, p0=p0, p1_=p1_, kb=kb: e.tensor_tensor(
                            kf[p0:p1_, s3, :], ps[p0:p1_, bank, :], bias[p0:p1_, kb, :], ALU.add), hm, kf_free[s3])
                        mm.read_by(i, h)
                        hk.append(h)
                    hn = rms_scale(kf[:rows, s3, :], rows, root(rows, square(kf[:rows, s3, :], rows, hk[-1])), [(p[0], p[1], p[5]) for p in parts])
                    if k_pending:
                        finish_k(*k_pending.pop())
                    elif q_left:
                        q_left.pop(0)()
                    sv = nvf % 2
                    nvf += 1
                    for p0, p1_, wk, wv, kb, knw, vb in parts:
                        bank, i, free = mm.take()
                        for kk in range(4):
                            hm = three(ps[:rows, bank, :], ch[:, s, kk, 128 * j:128 * j + rows], cl[:, s, kk, 128 * j:128 * j + rows],
                                       Wh[wv][:, kk, :], Wl[wv][:, kk, :], kk == 0, kk == 3, *wsplit[wv], *free)
                        h = DVE.do(lambda e, sv=sv, bank=bank, p0=p0, p1_=p1_, vb=vb: e.tensor_tensor(
                            vf[p0:p1_, sv, :], ps[p0:p1_, bank, :], bias[p0:p1_, vb, :], ALU.add), hm, vf_free[sv])
                        mm.read_by(i, h)
                    vf_free[sv] = SP.dma(s_v[sv], lambda e, b=b, t=t, rows=rows, sv=sv: e.dma_start(
                        Vd[b, 128 * t:128 * t + rows, :], vf[:rows, sv, :]), h)
                    ch_free[s] = hm
                    if q_left:
                        q_left.pop(0)()
                    k_pending.append((b, c, j, rows, s, s3, hn, j == 1 or c == 6, n if c < 6 else 66))
                    if units0:
                        for _ in range(2):
                            units0.pop(0)()
                        if not units0:
                            negated0()
                            rows0_due = True
                    elif rows0_due:
                        rows0()
                        rows0_due = False
                    if t < 4:
                        k = 4 * b + t
                        h_xb.append(DVE.do(lambda e: e.scalar_tensor_tensor(acc[:, k, :], obb, tg[:, 0:1], acc[:, k, :], ALU.mult, ALU.add), h_ob, h_tg, *h_xn.values()))
        finish_k(*k_pending.pop())
        if rows0_due:
            rows0()
        p1.close()
        barrier(*s_st, *s_v)

        NX = 12
        ORDER = [8, 9, 10, 11] + list(range(NE))
        s_gu = slot("s_gu")
        guh, gul = [in_kst0(0, 4, 512)], [in_kst0(2048, 4, 512)]
        dnh, dnl = [in_kst0(4096, 2, 512)], [in_kst0(5120, 2, 512)]
        wx_free = [[], []]
        h_wx = {}

        def weights_of(x):
            def piece(k, q, part):
                if k == 4:
                    w = ap["w_down"][x] if x < NE else ap["w_sh_down"][256 * (x - NE):256 * (x - NE) + 256, :]
                    return w.rearrange("(k p) h -> p k h", p=128)[:, :, 256 * q:256 * q + 256]
                w = ap["w_gate_up"][x] if x < NE else ap["w_sh_gate_up"]
                c0 = 256 * q if x < NE else 1024 * q + 256 * (x - NE)
                return w.rearrange("(k p) f -> p k f", p=128)[:, k:k + part, c0:c0 + 256]
            return piece

        def early_piece(k):
            dst = Vg[0][:, 0:8, :].rearrange("p a b -> p (a b)").rearrange("p (k n) -> p k n", k=2)
            src = weights_of(ORDER[0])
            for q in range(2):
                h = SP.dma(s_gu, lambda e: e.dma_start(dst[:, :, 256 * q:256 * q + 256], src(k, q, 2)), *vg_free[0], *kst_free[0][1])

            def split():
                hi, lo = (guh[0][:, k:k + 2], gul[0][:, k:k + 2]) if k < 4 else (dnh[0], dnl[0])
                a = ACTQ.do(lambda e: e.activation(hi, dst, ACT.Copy), h)
                b_ = DVE.do(lambda e: e.tensor_tensor(lo, dst, hi.bitcast(F32), ALU.subtract), a)
                vg_free[0] = [a, b_]
                h_wx[0] = [a, b_]
            return split

        p2 = ExitStack()
        Kst.append(sb(p2, "Kst1", [128, 4, NKP], F32R))
        Qst += [sb(p2, f"Qst{i}", [128, 4, LQ], F32R) for i in (1, 2)]
        Vg = [sb(p2, f"Vg{i}", [128, NKT, 128], F32) for i in range(2)]
        P = [sb(p2, f"P{i}", [128, 4, LQ], F32) for i in range(4)]
        ones = sb(p2, "ones", [128, 32], F32)
        sacc = sb(p2, "sacc", [128, 4, LQ], F32)
        aTh = sb(p2, "aTh", [128, 4, LQ], F32R)
        aTl = sb(p2, "aTl", [128, 4, LQ], F32R)
        Woh = sb(p2, "Woh", [128, 4, D], F32R)
        Wol = sb(p2, "Wol", [128, 4, D], F32R)
        rt2 = sb(p2, "rt", [128, 2, D], F32)
        ot2 = sb(p2, "ot", [128, 2, D], F32)
        oi = sb(p2, "oi", [128, D], F32)
        si = sb(p2, "si", [128, D], F32)

        load_values(0)
        h_indk.append(SP.dma(s_c2, lambda e: e.dma_start(Kst[1][96:100].bitcast(F32), Kst[0][96:100].bitcast(F32))))
        load_keys(1, 0)
        load_queries(1)
        load_keys(1, 1)
        SP.wait(*[(q.sem, q.n) for q in (*s_st, *s_v)])
        for i, dst in enumerate((ot2, rt2)):
            h_wo = SP.dma(s_wo, lambda e: e.dma_start(dst[:], ap["o_wT"].rearrange("(k p) o -> p k o", p=128)[:, 2 * i:2 * i + 2, :]))
        load_queries(2)
        load_values(1)
        h_ones = DVE.do(lambda e: e.memset(ones[:], 1.0))
        h_wos = []

        def split_wo():
            for i, src in enumerate((ot2, rt2)):
                k = slice(2 * i, 2 * i + 2)
                a = ACTQ.do(lambda e: e.activation(Woh[:, k], src[:], ACT.Copy), h_wo)
                h_wos.append(POOL.do(lambda e: e.tensor_tensor(Wol[:, k], src[:], Woh[:, k].bitcast(F32), ALU.subtract), a))
            shared["ot", -2] = shared["ot", -1] = h_wos[1]

        rb = Banks([2, 3, 4])
        ra.banks.append(5)
        ra.readers.append([])
        p_free = [[], [], [], []]
        ON_POOL = (0, 1, 2, 4, 6, 7, 8)
        FIRST = min(t for t in range(10) if t not in ON_POOL)
        shared = {"sacc": None, 6: [], 7: [], "a": []}

        def project_tile(b, t, h6):
            k = 4 * b + t
            bank, i, free = ra.take()
            for kk in range(4):
                h = three(ps[:, bank, :], aTh[:, kk, 128 * t:128 * t + 128], aTl[:, kk, 128 * t:128 * t + 128],
                          Woh[:, kk, :], Wol[:, kk, :], kk == 0, kk == 3, *h6, h_wos[1], *free)
            d = DVE.do(lambda e: e.scalar_tensor_tensor(acc[:, k, :], ps[:, bank, :], tg[:, 0:1], acc[:, k, :], ALU.mult, ALU.add), h, h_xb[k])
            ra.read_by(i, d)
            d = DVE.do(lambda e: e.bn_stats(st3[:, k, 0:6], acc[:, k, :]), d)
            h_st3[k] = DVE.do(lambda e: e.bn_aggr(st3[:, k, 6:8], st3[:, k, 0:6]), d)
            shared["a"] = [h]

        def group(G):
            g, s = G % 4, G % 2
            pslot, hexp, at_end = {}, {}, {}
            ot, rt = ot2[:, G % 2, :], rt2[:, G % 2, :]
            h_sacc = [None]

            def scores(kt, j):
                m = 128 if kt < 12 else 65
                if j == 0:
                    pslot[kt], hexp[kt] = (NKT * G + kt) % 4, []
                    ACTQ.wait(*p_free[pslot[kt]])
                    p_free[pslot[kt]] = []
                pt = P[pslot[kt]]
                bank, i, free = rb.take()
                h = PE.do(lambda e: e.matmul(ps[:m, bank, :], Kst[s][0:100, j, 128 * kt:128 * kt + m], Qst[G % 3][0:100, j, :],
                                             start=True, stop=True), h_k[G, int(kt > 9)], h_q[G], h_indk[s], mdone[G], *free)
                if kt == 9:
                    kst_free[s][0] = [h]
                if kt == 12:
                    kst_free[s][1] = qst_free[G % 3] = [h]
                h = ACTQ.do(lambda e: e.activation(pt[:m, j, :], ps[:m, bank, :], ACT.Exp, scale=SCALE), h)
                rb.read_by(i, h)
                hexp[kt].append(h)

            def heads(bank, w, pt, p0, p1_, first, last, *waits):
                for j in range(4):
                    h = PE.do(lambda e: e.matmul(ps[32 * j:32 * j + 32, bank, :], w(j), pt[p0:p1_, j, :], start=first, stop=last,
                                                 tile_position=(p0, 32 * j)), *waits, *(shared[bank] if first else []), mark=(j == 3))
                return h

            def weigh(kt, p0, p1_, first, last):
                h = heads(6, lambda j: Vg[s][p0:p1_, kt, 32 * j:32 * j + 32], P[pslot[kt]], p0, p1_, first, last, h_v[G], *hexp[kt])
                p_free[pslot[kt]].append(h)
                return h

            def total(kt, p0, p1_, first, last):
                h = heads(7, lambda j: ones[p0:p1_, :], P[pslot[kt]], p0, p1_, first, last, h_ones, *hexp[kt])
                p_free[pslot[kt]].append(h)
                return h

            def add_on_pool(kt):
                i = ON_POOL.index(kt)
                if i == 0:
                    return
                x = P[pslot[ON_POOL[0]]] if i == 1 else sacc
                w = hexp[ON_POOL[0]] if i == 1 else [h_sacc[0]]
                h = h_sacc[0] = POOL.do(lambda e: e.tensor_tensor(sacc[:], x[:], P[pslot[kt]][:], ALU.add), *w, *hexp[kt], shared["sacc"])
                for k in (kt, ON_POOL[0])[:2 if i == 1 else 1]:
                    p_free[pslot[k]].append(h)

            def pool_total():
                h = heads(7, lambda j: ones[:, :], sacc, 0, 128, False, True, h_sacc[0])
                shared["sacc"] = h
                h1 = ACTQ.do(lambda e: e.activation(ot, ps[:, 6, :], ACT.Copy), h, shared.get(("ot", G - 2)))
                h2 = ACTQ.do(lambda e: e.activation(rt, ps[:, 7, :], ACT.Copy), h, shared.get(("ot", G - 2)))
                shared[6], shared[7] = [h1], [h2]
                at_end["txt"] = h2

            def end(h):
                h2 = at_end["txt"]
                if G == NG - 1:
                    last_end(h, h2)
                    return
                h7 = ACTQ.do(lambda e: e.activation(si[:], ps[:, 7, :], ACT.Copy), h, shared.get("si"))
                h1 = DVE.do(lambda e: e.tensor_tensor(oi[:], ps[:, 6, :], rt, ALU.mult), h, h2, *shared.get("h6", []))
                h3 = POOL.do(lambda e: e.tensor_tensor(ot, ot, si[:], ALU.mult), h7, h2)
                h4 = shared["si"] = POOL.do(lambda e: e.tensor_tensor(rt, rt, si[:], ALU.mult), h1, h3)
                shared[6], shared[7] = [h1], [h7]
                hr, out = [], []

                def inverse(c):
                    cs = slice(128 * c, 128 * c + 128)
                    hr.append(DVE.do(lambda e: e.reciprocal(rt[:, cs], rt[:, cs]), h4))

                def normalise():
                    hc = POOL.do(lambda e: e.tensor_tensor(oi[:], oi[:], ot, ALU.add), h1, h3)
                    hd = POOL.do(lambda e: e.tensor_tensor(oi[:], oi[:], rt, ALU.mult), hc, hr[-1])
                    shared["ot", G] = hd
                    out.append(hd)

                def split():
                    he = ACTQ.do(lambda e: e.activation(aTh[:, g, :], oi[:], ACT.Copy), out[0], *shared["a"])
                    hf = POOL.do(lambda e: e.tensor_tensor(aTl[:, g, :], oi[:], aTh[:, g, :].bitcast(F32), ALU.subtract), he, *shared["a"])
                    shared["h6"] = [he, hf]

                base = NKT * (G + 1)
                later[base + 11] += [lambda c=c: inverse(c) for c in range(4)]
                later[base + 12] += [normalise]
                later[base + 13] += [split]
                if g == 3:
                    for t in range(4):
                        later[base + 14 + t // 2] += [lambda t=t: project_tile(G // 4, t, shared["h6"])]

            def last_end(h, h2):
                for t in range(4):
                    cs = slice(128 * t, 128 * t + 128)
                    a = DVE.do(lambda e: e.tensor_tensor(oi[:, cs], ps[:, 6, cs], rt[:, cs], ALU.mult), h, h2, *shared.get("h6", []))
                    b_ = DVE.do(lambda e: e.tensor_tensor(rt[:, cs], rt[:, cs], ps[:, 7, cs], ALU.mult), a)
                    c = DVE.do(lambda e: e.tensor_tensor(ot[:, cs], ot[:, cs], ps[:, 7, cs], ALU.mult), h2)
                    b_ = DVE.do(lambda e: e.reciprocal(rt[:, cs], rt[:, cs]), b_)
                    a = DVE.do(lambda e: e.tensor_tensor(oi[:, cs], oi[:, cs], ot[:, cs], ALU.add), a, c)
                    a = DVE.do(lambda e: e.tensor_tensor(oi[:, cs], oi[:, cs], rt[:, cs], ALU.mult), a, b_)
                    he = ACTQ.do(lambda e: e.activation(aTh[:, g, cs], oi[:, cs], ACT.Copy), a, *shared["a"])
                    hf = DVE.do(lambda e: e.tensor_tensor(aTl[:, g, cs], oi[:, cs], aTh[:, g, cs].bitcast(F32), ALU.subtract), he, *shared["a"])
                    if t:
                        project_tile(NB - 1, t - 1, before)
                    before = [he, hf]
                project_tile(NB - 1, 3, before)

            return scores, weigh, total, add_on_pool, pool_total, end

        h_rs = {}

        def root_of_variance(b):
            v = st3[:, 4 * b:4 * b + 4, :]
            a = DVE.do(lambda e: e.tensor_scalar(v[:, :, 8], v[:, :, 7], 1e-5, None, ALU.add), h_st3[4 * b + 3])
            c = ACTQ.do(lambda e: e.activation(v[:, :, 9], v[:, :, 8], ACT.Sqrt), a)
            h_rs[b] = DVE.do(lambda e: e.reciprocal(v[:, :, 10], v[:, :, 9]), c)

        later = [[] for _ in range(NKT * NG + 2)]
        for i in range(3):
            later[NKT * (NG - 1) + 2 + 3 * i].append(lambda i=i: first_split.append(early_piece(2 * i)))
            later[NKT * (NG - 1) + 4 + 3 * i].append(lambda: first_split.pop()())
        later[NKT * NG] += [lambda b=b: root_of_variance(b) for b in range(NB - 1)]
        first_split = []
        later[6].append(split_wo)
        units = []
        UST, UEND = 0, 11
        for step in range(NKT * NG + 2):
            G, kt = divmod(step, NKT)
            if kt == 0 and G < NG:
                cur = group(G)
                if G + 1 < NG:
                    units, negated, rows = max_units(G + 1)
            quota = -(-len(units) // (UEND - kt)) if (UST if G else 3) <= kt < UEND else 0
            unit_calls = 7

            def unit():
                nonlocal quota, unit_calls
                n = -(-quota // unit_calls)
                unit_calls -= 1
                quota -= n
                for _ in range(n):
                    units.pop(0)()
                    if not units:
                        negated()

            late = False
            if step >= 2:
                pG, pk = divmod(step - 2, NKT)
                if pk == 0:
                    past = cur
                late = pk in (0, 10)
                _, weigh, total, add_on_pool, pool_total, end = past
            def weighing():
                if step >= 2:
                    weigh(pk, 64 if pk == 10 else 0, 65 if pk == 12 else 128, pk in (0, 10), pk == 12)
                    if pk == 9:
                        weigh(10, 0, 64, False, True)

            def totalling():
                if step < 2:
                    return
                if pk < 10 and pk not in ON_POOL:
                    total(pk, 0, 128, pk == FIRST, False)
                if pk == 9:
                    total(10, 0, 64, False, False)
                    pool_total()
                if pk == 10:
                    total(10, 64, 128, True, False)
                if pk == 11:
                    total(11, 0, 128, False, False)
                if pk == 12:
                    h = total(12, 0, 65, False, True)
                    vg_free[pG % 2] = [h]
                    end(h)
                    if pG + 2 < NG:
                        load_values(pG + 2)

            def score(j):
                if G < NG:
                    cur[0](kt, j)
                    if j == 3 and kt - 1 in ON_POOL:
                        cur[3](kt - 1)

            if kt == 0:
                weighing()
                unit()
                totalling()
                unit()
                unit()
                for j in range(4):
                    score(j)
                    unit()
            else:
                score(0)
                unit()
                score(1)
                unit()
                if kt == 12 and G + 1 < NG:
                    rows()
                if not late:
                    weighing()
                unit()
                score(2)
                unit()
                score(3)
                unit()
                if late:
                    weighing()
                totalling()
                unit()
            while later[step]:
                later[step].pop(0)()
            if kt:
                unit()
            if kt == 10 and G + 2 < NG:
                load_keys(G + 2, 0)
            if kt == 12 and G + 2 < NG:
                load_keys(G + 2, 1)
                if G + 3 < NG:
                    load_queries(G + 3)
        root_of_variance(NB - 1)
        p2.close()
        barrier()

        p3 = ExitStack()
        xTh = sb(p3, "xTh", [128, 4, 2048], F32R)
        xTl = sb(p3, "xTl", [128, 4, 2048], F32R)
        guh.append(sb(p3, "guh1", [128, 4, 512], F32R)[:])
        gul.append(sb(p3, "gul1", [128, 4, 512], F32R)[:])
        dnh.append(sb(p3, "dnh1", [128, 2, 512], F32R)[:])
        dnl.append(sb(p3, "dnl1", [128, 2, 512], F32R)[:])
        gur = sb(p3, "gur", [128, 4, 512], F32)
        dnr = sb(p3, "dnr", [128, 2, 512], F32)
        raw3_free = []

        def load_expert(n):
            nonlocal raw3_free
            s, src = n % 2, weights_of(ORDER[n])
            if ORDER[n] < NE:
                SP.dma(s_gu, lambda e: e.dma_start(gur[:], ap["w_gate_up"][ORDER[n]].rearrange("(k p) f -> p k f", p=128)), *raw3_free)
                h = SP.dma(s_gu, lambda e: e.dma_start(dnr[:], ap["w_down"][ORDER[n]].rearrange("(k p) h -> p k h", p=128)))
            else:
                y = ORDER[n] - NE
                for q in range(2):
                    SP.dma(s_gu, lambda e: e.dma_start(gur[:, :, 256 * q:256 * q + 256], src(0, q, 4)), *raw3_free)
                h = SP.dma(s_gu, lambda e: e.dma_start(dnr[:], ap["w_sh_down"][256 * y:256 * y + 256, :].rearrange("(k p) h -> p k h", p=128)))
            a = ACTQ.do(lambda e: e.activation(guh[s], gur[:], ACT.Copy), h, *wx_free[s])
            b_ = ACTQ.do(lambda e: e.activation(dnh[s], dnr[:], ACT.Copy))
            c = POOL.do(lambda e: e.tensor_tensor(gul[s], gur[:], guh[s].bitcast(F32), ALU.subtract), a)
            d = POOL.do(lambda e: e.tensor_tensor(dnl[s], dnr[:], dnh[s].bitcast(F32), ALU.subtract), b_)
            raw3_free = [a, b_, c, d]
            h_wx[n] = [a, b_, c, d]

        ah = [Qst[0][:, 0:2, :], Qst[0][:, 2:4, :]]
        al = [sb(p3, f"al{i}", [128, 2, 512], F32R) for i in range(2)]
        sg = sb(p3, "sg", [128, 2, 512], F32)
        af = sb(p3, "af", [128, 2, 512], F32)
        xn3 = sb(p3, "xn3", [128, 2, D], F32)
        gtr = sb(p3, "gtr", [128, 4, NE], F32)
        gth = sb(p3, "gth", [128, 4, NE], F32R)
        gtl = sb(p3, "gtl", [128, 4, NE], F32R)
        iot = sb(p3, "iot", [128, NE], F32)
        lrow = sb(p3, "lrow", [NE, 4, 512], F32)
        cmb = sb(p3, "cmb", [128, 16, NE], F32)
        lg = sb(p3, "lg", [128, 16, NE], F32)
        lm = sb(p3, "lm", [128, 16, NE], F32)
        li = sb(p3, "li", [128, 16, NE], U32)
        wt = sb(p3, "wt", [128, 16, 8], F32)

        s_c3, s_out = slot("s_c3"), slot("s_out")
        SP.dma(s_c3, lambda e: e.dma_start(iot[:], ap["iota8"]))
        h_gt = SP.dma(s_c3, lambda e: e.dma_start(gtr[:], ap["w_gate"].rearrange("(k p) n -> p k n", p=128)))

        tr3 = Banks([5, 6])
        h_xt, xn3_free, h_xn3 = {}, [None] * 2, {}

        def normed(k):
            xs = k % 2
            h_xn3[k] = DVE.do(lambda e: e.tensor_scalar(xn3[:, xs, :], acc[:, k, :], st3[:, k, 6:7], st3[:, k, 10:11], ALU.subtract, ALU.mult), h_rs[k // 4], xn3_free[xs])

        def across(k):
            xs = k % 2
            bank, i, free = tr3.take()
            for g in range(4):
                h = PE.do(lambda e: e.transpose(ps[:, bank, 128 * g:128 * g + 128], xn3[:, xs, 128 * g:128 * g + 128], ident[:]), h_xn3[k], *free, mark=(g == 3))
            xn3_free[xs] = h
            v = ps[:, bank, :].rearrange("p (g s) -> p g s", g=4)
            hi, lo = xTh[:, :, 128 * k:128 * k + 128], xTl[:, :, 128 * k:128 * k + 128]
            a = ACTQ.do(lambda e: e.activation(hi, v, ACT.Copy), h)
            if k + 2 < 16:
                normed(k + 2)
            d = DVE.do(lambda e: e.tensor_sub(lo, v, hi.bitcast(F32)), a)
            tr3.read_by(i, a)
            tr3.read_by(i, d)
            h_xt[k] = (a, d)

        normed(0)
        normed(1)
        for k in range(4):
            across(k)
        a = ACTQ.do(lambda e: e.activation(gth[:], gtr[:], ACT.Copy), h_gt)
        h_gts = DVE.do(lambda e: e.tensor_sub(gtl[:], gtr[:], gth[:].bitcast(F32)), a)
        h_lg = []

        def route(tb):
            bank, i, free = up3.take()
            for kk in range(4):
                h = three(ps[0:NE, bank, :], gth[:, kk, :], gtl[:, kk, :], xTh[:, kk, 512 * tb:512 * tb + 512], xTl[:, kk, 512 * tb:512 * tb + 512],
                          kk == 0, kk == 3, *h_xt[4 * tb + 3], h_gts, *free)
            d = DVE.do(lambda e: e.tensor_copy(lrow[:, tb, :], ps[0:NE, bank, :]), h)
            up3.read_by(i, d)
            return d

        def logits_across(tb, d):
            for t in range(4):
                k = 4 * tb + t
                h_lg.append(PE.do(lambda e: e.transpose(ps[:, 7, NE * k:NE * k + NE], lrow[:, tb, 128 * t:128 * t + 128], ident[0:NE, 0:NE]), d))

        comb = {}

        def combine(stage):
            nonlocal h_cmb
            a = comb.get("h")
            if stage == 0:
                a = DVE.do(lambda e: e.tensor_copy(lg[:].rearrange("p k n -> p (k n)"), ps[:, 7, 0:16 * NE]), h_lg[-1])
                for k in range(16):
                    m = DVE.do(lambda e: e.max(lm[:, k, :], lg[:, k, :]), a)
                comb["h"] = m
            elif stage == 1:
                for k in range(16):
                    m = DVE.do(lambda e: e.max_index(li[:, k, :], lm[:, k, :], lg[:, k, :]), a)
                comb["h"] = m
            elif stage == 2:
                a = DVE.do(lambda e: e.tensor_sub(wt[:, :, 0], lm[:, :, 1], lm[:, :, 0]), a)
                c = ACTQ.do(lambda e: e.activation(wt[:, :, 1], wt[:, :, 0], ACT.Exp), a)
                a = DVE.do(lambda e: e.tensor_scalar(wt[:, :, 2], wt[:, :, 1], 1.0, None, ALU.add), c)
                a = DVE.do(lambda e: e.reciprocal(wt[:, :, 3], wt[:, :, 2]), a)
                a = DVE.do(lambda e: e.tensor_scalar(wt[:, :, 4], wt[:, :, 3], tg[:, 1:2], None, ALU.mult), a)
                a = DVE.do(lambda e: e.tensor_tensor(wt[:, :, 5], wt[:, :, 4], wt[:, :, 1], ALU.mult), a)
                comb["h"] = DVE.do(lambda e: e.tensor_copy(wt[:, :, 6:8], li[:, :, 0:2]), a)
            elif stage == 3:
                for k in range(16):
                    m = DVE.do(lambda e: e.tensor_scalar(lg[:, k, :], iot[:], wt[:, k, 7:8], wt[:, k, 5:6], ALU.is_equal, ALU.mult), a, h_gt)
                comb["d"] = m
            else:
                for k in range(16):
                    m = DVE.do(lambda e: e.tensor_scalar(cmb[:, k, :], iot[:], wt[:, k, 6:7], wt[:, k, 4:5], ALU.is_equal, ALU.mult), a)
                h_cmb = DVE.do(lambda e: e.tensor_tensor(cmb[:], cmb[:], lg[:], ALU.add), m, comb["d"])

        h_cmb = None

        up3, dn3 = Banks([0, 1, 2]), Banks([3, 4])
        a_free3 = [[], []]
        sg_free, af_free = [None] * 2, [[] for _ in range(2)]
        pend = None
        acc_last = [None] * 16
        nstep = 0

        def down(n, tb, s, hact):
            x, w = ORDER[n], n % 2
            for t in range(4):
                bank, i, free = dn3.take()
                k = 4 * tb + t
                for kk in range(2):
                    h = three(ps[:, bank, :], ah[s][:, kk, 128 * t:128 * t + 128], al[s][:, kk, 128 * t:128 * t + 128],
                              dnh[w][:, kk, :], dnl[w][:, kk, :], kk == 0, kk == 1, *hact, *h_wx[n], *free)
                sc = cmb[:, k, x:x + 1] if x < NE else tg[:, 1:2]
                d = DVE.do(lambda e: e.scalar_tensor_tensor(acc[:, k, :], ps[:, bank, :], sc, acc[:, k, :], ALU.mult, ALU.add), h, acc_last[k], h_xn3[k], h_cmb)
                dn3.read_by(i, d)
                acc_last[k] = d
            a_free3[s] = [h]
            if tb == 3:
                wx_free[w] = [h]
                if n + 2 < NX:
                    load_expert(n + 2)
            if n == NX - 1:
                for t in range(4):
                    k = 4 * tb + t
                    SP.dma(s_out, lambda e, k=k: e.dma_start(ap["out"].rearrange("b (t p) d -> p (b t) d", p=128)[:, k, :], acc[:, k, :]), acc_last[k])

        load_expert(1)
        for n, x in enumerate(ORDER):
            w = n % 2
            if n == 1:
                for z, i in ((up3, 0), (dn3, 1)):
                    z.banks.append(tr3.banks[i])
                    z.readers.append(tr3.readers[i])
            for tb in range(4):
                s = nstep % 2
                nstep += 1
                hact = []
                for f in range(2):
                    got = []
                    for half in range(2):
                        bank, i, free = up3.take()
                        c0 = 256 * half + 128 * f
                        for kk in range(4):
                            h = three(ps[:, bank, :], guh[w][:, kk, c0:c0 + 128], gul[w][:, kk, c0:c0 + 128],
                                      xTh[:, kk, 512 * tb:512 * tb + 512], xTl[:, kk, 512 * tb:512 * tb + 512], kk == 0, kk == 3,
                                      *h_wx[n], *h_xt[4 * tb + 3], *free)
                        got.append((bank, i, h))
                        if n == 0 and tb < 3:
                            for k in ((0,), (1, 2), (3,), ())[2 * f + half]:
                                across(4 * (tb + 1) + k)
                    (bg, ig, hg), (bu, iu, hu) = got
                    a = ACTQ.do(lambda e, f=f, bg=bg: e.activation(sg[:, f, :], ps[:, bg, :], ACT.Silu), hg, sg_free[f])
                    up3.read_by(ig, a)
                    d = DVE.do(lambda e, f=f, bu=bu: e.tensor_tensor(af[:, f, :], sg[:, f, :], ps[:, bu, :], ALU.mult), a, hu, *af_free[f])
                    up3.read_by(iu, d)
                    sg_free[f] = d
                    c = ACTQ.do(lambda e, f=f, s=s: e.activation(ah[s][:, f, :], af[:, f, :], ACT.Copy), d, *a_free3[s])
                    g_ = DVE.do(lambda e, f=f, s=s: e.tensor_sub(al[s][:, f, :], af[:, f, :], ah[s][:, f, :].bitcast(F32)), c, *a_free3[s])
                    af_free[f] = [g_]
                    hact += [c, g_]
                if pend:
                    down(*pend)
                if n == 0:
                    d = route(tb)
                    if tb:
                        logits_across(tb - 1, d_route)
                    d_route = d
                if n == 1 and tb == 0:
                    logits_across(3, d_route)
                if 5 <= nstep - 1 < 10:
                    combine(nstep - 6)
                pend = (n, tb, s, hact)
        down(*pend)
        SP.wait((s_out.sem, s_out.n))
        for s in slots:
            SP.wait((s.sem, s.n))

        p3.close()


def kernel(**inputs):
    import concourse.bacc as _bacc
    from concourse.bass_utils import run_bass_kernel_spmd as _run

    def X(n):
        return np.asarray(inputs[n])

    c = X("ctx_2048")
    ctxT = np.ascontiguousarray(np.concatenate([c[:, NIMG:], c[:, :NIMG]], axis=1).transpose(0, 2, 1))
    ind = np.zeros((4, NKP), np.float32)
    ind[0:2, :NTXT] = 1.0
    ind[2:4, NTXT:] = 1.0
    arrays = {
        "x": X("x"), "ctxT": ctxT, "g_xattn": X("g_xattn"), "g_ffn": X("g_ffn"),
        "ident": np.eye(128, dtype=np.float32), "ind": ind,
        "iota8": np.ascontiguousarray(np.broadcast_to(np.arange(8, dtype=np.float32), (128, 8))),
        "w_gate": X("L0_ffn_w_gate"), "w_gate_up": X("L0_ffn_w_gate_up"), "w_down": X("L0_ffn_w_down"),
        "w_sh_gate_up": X("L0_ffn_w_sh_gate_up"), "w_sh_down": X("L0_ffn_w_sh_down"),
    }
    for n in ("q_b", "k_b", "v_b", "k_img_b", "v_img_b", "o_b", "norm_q_w", "norm_k_w", "norm_k_img_w"):
        arrays[n] = X("L0_xattn_" + n)
    for n in ("q_w", "k_w", "v_w", "k_img_w", "v_img_w", "o_w"):
        arrays[n + "T"] = np.ascontiguousarray(X("L0_xattn_" + n).T)

    nc = _bacc.Bacc("TRN2", target_bir_lowering=False, num_devices=1)
    ins, ap = {}, {}
    for name, a in arrays.items():
        a = np.ascontiguousarray(a)
        ins["in_" + name] = a
        ap[name] = nc.dram_tensor("in_" + name, a.shape, mybir.dt.from_np(a.dtype), kind="ExternalInput").ap()
    ap["out"] = nc.dram_tensor("out_0", (NB, LQ, D), F32, kind="ExternalOutput").ap()
    flamingo_program(nc, ap)
    r = _run(nc, [ins], core_ids=[0])
    return r.results[0]["out_0"]
```
